# Optimizing a Trainium2 kernel written in Bass

```python
import numpy as np
import jax
import jax.numpy as jnp

def _softmax(x, axis=-1):
    return jax.nn.softmax(x, axis=axis)

def _gelu(x):
    return jax.nn.gelu(x, approximate=True)

def _silu(x):
    return jax.nn.silu(x)

def _sigmoid(x):
    return jax.nn.sigmoid(x)

def _layernorm(x, axis=-1, eps=1e-05):
    m = jnp.mean(x, axis=axis, keepdims=True)
    v = jnp.var(x, axis=axis, keepdims=True)
    return (x - m) / jnp.sqrt(v + eps)

def _scatter_add(tgt, idx, src, axis=0):
    return tgt.at[idx].add(src)

def _segment_sum(src, seg, n):
    return jax.ops.segment_sum(src, seg, n)
kernel_name = 'mk_rec_standalone_d1_rec_r8_5ce131'

def setup_inputs(seed: int=0):
    np.random.seed(seed)
    _w = jnp.asarray

    def _rec_inputs():
        import jax
        import jax.numpy as jnp
        _rk = jax.random.key(seed)
        r_inputs = -0.00171016 + 1.00035 * jax.random.normal(jax.random.fold_in(_rk, 1), (512, 40, 32), jnp.float32)
        return r_inputs
    r_inputs = _rec_inputs()

    def _L0_rec_setup():
        import jax, jax.numpy as jnp
        import numpy as np
        B, F0, K = (256, 40, 32)
        CIN_SIZE = [200, 200]

        def _cin(inputs, params):
            Bb, F0_, Kk = inputs.shape
            res = inputs
            outs = []
            for wq, wk, wv, cw in params:
                x0_wk = inputs * wk
                x0_wv = inputs * wv
                xi_wq = res * wq
                phi = jnp.einsum('bfk,bgk->bkfg', x0_wk, xi_wq)
                alpha = jax.nn.softmax(phi, axis=2)
                x = alpha * jnp.transpose(x0_wv, (0, 2, 1))[:, :, :, None]
                x = x.reshape(Bb, Kk, -1)
                out = jnp.einsum('bkc,cj->bjk', x, cw[0])
                outs.append(out)
                res = out
            cat = jnp.concatenate(outs, axis=1)
            return cat.sum(axis=-1)
        key = jax.random.key(seed)
        ks = jax.random.split(key, 1 + 4 * len(CIN_SIZE))
        field_num = [F0] + CIN_SIZE
        d = {'inputs': jax.random.normal(ks[0], (B, F0, K), dtype=jnp.float32)}
        for i in range(len(CIN_SIZE)):
            d[f'wq{i}'] = jax.random.normal(ks[1 + 4 * i], (1, field_num[i], K), dtype=jnp.float32) * 0.05
            d[f'wk{i}'] = jax.random.normal(ks[2 + 4 * i], (1, F0, K), dtype=jnp.float32) * 0.05
            d[f'wv{i}'] = jax.random.normal(ks[3 + 4 * i], (1, F0, K), dtype=jnp.float32) * 0.05
            lim = (6.0 / (F0 * field_num[i] + field_num[i + 1])) ** 0.5
            d[f'cw{i}'] = jax.random.uniform(ks[4 + 4 * i], (1, F0 * field_num[i], field_num[i + 1]), minval=-lim, maxval=lim, dtype=jnp.float32)
        return d
    _L0_rec_all = _L0_rec_setup()
    _L0_rec_in = {k: v for k, v in _L0_rec_all.items() if k in ('wq0', 'wk0', 'wv0', 'cw0', 'wq1', 'wk1', 'wv1', 'cw1')}
    del _L0_rec_all
    return {'r_inputs': r_inputs, 'L0_rec_wq0': _L0_rec_in['wq0'], 'L0_rec_wk0': _L0_rec_in['wk0'], 'L0_rec_wv0': _L0_rec_in['wv0'], 'L0_rec_cw0': _L0_rec_in['cw0'], 'L0_rec_wq1': _L0_rec_in['wq1'], 'L0_rec_wk1': _L0_rec_in['wk1'], 'L0_rec_wv1': _L0_rec_in['wv1'], 'L0_rec_cw1': _L0_rec_in['cw1']}

def reference(r_inputs, L0_rec_wq0, L0_rec_wk0, L0_rec_wv0, L0_rec_cw0, L0_rec_wq1, L0_rec_wk1, L0_rec_wv1, L0_rec_cw1):
    import jax
    import jax.numpy as jnp

    def _L0_rec_ref(inputs, wq0, wk0, wv0, cw0, wq1, wk1, wv1, cw1):
        import jax, jax.numpy as jnp
        import numpy as np
        B, F0, K = (256, 40, 32)
        CIN_SIZE = [200, 200]

        def _cin(inputs, params):
            Bb, F0_, Kk = inputs.shape
            res = inputs
            outs = []
            for wq, wk, wv, cw in params:
                x0_wk = inputs * wk
                x0_wv = inputs * wv
                xi_wq = res * wq
                phi = jnp.einsum('bfk,bgk->bkfg', x0_wk, xi_wq)
                alpha = jax.nn.softmax(phi, axis=2)
                x = alpha * jnp.transpose(x0_wv, (0, 2, 1))[:, :, :, None]
                x = x.reshape(Bb, Kk, -1)
                out = jnp.einsum('bkc,cj->bjk', x, cw[0])
                outs.append(out)
                res = out
            cat = jnp.concatenate(outs, axis=1)
            return cat.sum(axis=-1)
        return _cin(inputs, [(wq0, wk0, wv0, cw0), (wq1, wk1, wv1, cw1)])
    y = _L0_rec_ref(r_inputs, L0_rec_wq0, L0_rec_wk0, L0_rec_wv0, L0_rec_cw0, L0_rec_wq1, L0_rec_wk1, L0_rec_wv1, L0_rec_cw1)
    return y

_drawn_inputs = setup_inputs


def setup_inputs(seed=0):
    import zlib

    import numpy as np

    out = dict(_drawn_inputs(seed))
    spreads = {}
    factors = {'L0_rec_wq0': 8.0, 'L0_rec_wk0': 8.0, 'L0_rec_wq1': 64.0, 'L0_rec_wk1': 64.0}
    for name, (base, spread) in spreads.items():
        noise = np.random.default_rng([zlib.crc32(name.encode()), seed]).standard_normal(out[name].shape)
        drawn = base * np.exp(spread * noise) if base else spread * noise
        out[name] = jnp.asarray(drawn.astype(out[name].dtype))
    for name, factor in factors.items():
        out[name] = (out[name] * factor).astype(out[name].dtype)
    return out
```

```python
import concourse.bass as bass
from concourse import mybir
from contextlib import ExitStack

B, F, K, J = 512, 40, 32, 200
G = J
P = 128
TILES = B * K // P
BT = P // K
KH = 16
U = P // KH
FA, FB = 5, 8
GU = 4
NA = 6
C0 = F * F
CH0 = 124
NCH0 = -(-C0 // CH0)
C1, CH1 = F * G, 125
NCH1 = C1 // CH1
CHUNKS = FA * 2
ARG_BANK = [0, 1, 2, 0, 1, 2, 0, 1, 2, 1]
ARG_BACK = [4, 2, 4, 3, 3, 3, 3, 3, 3, 2]
EW_LEAD, SB_LEAD = 3, 2
EW_STEPS, Q_STEPS = 8, 11


def cin_kernel(nc, x_rows, x_units, w_rows, wv_units, cw0, cw1, ident_d, diag_a, sum_f, bcast_k, sum_k, fb_mask, out):
    f32, bf16 = mybir.dt.float32, mybir.dt.bfloat16
    ALU, ACT, AX = mybir.AluOpType, mybir.ActivationFunctionType, mybir.AxisListType

    with ExitStack() as ctx:
        def sb(name, shape, dt=f32):
            return ctx.enter_context(nc.sbuf_tensor(name, shape, dt))

        def pb(name, shape):
            return ctx.enter_context(nc.psum_tensor(name, shape, f32))

        def sem(name):
            return ctx.enter_context(nc.semaphore(name))

        a_parts = nc.dram_tensor("a_parts", (3, P, TILES * F), bf16, kind="Internal").ap()
        q_parts = nc.dram_tensor("q_parts", (2, 5, P, G), bf16, kind="Internal").ap()
        z_dram = nc.dram_tensor("z_dram", (B, F, G), f32, kind="Internal").ap()

        xr = sb("xr", [P, TILES * F])
        xu = sb("xu", [P, 2, U * FA])
        w_sb = sb("w_sb", [P, 5, G])
        wvu = sb("wvu", [P, 2, FA])
        wv_mask = sb("wv_mask", [P, 2, FA, FB])
        fbm = sb("fbm", [P, FB])
        cw0_sb = sb("cw0_sb", [P, NCH0, J])
        big = sb("big", [P, NCH1, J])
        ident = sb("ident", [P, P])
        dga = sb("dga", [P, KH], bf16)
        ones_f = sb("ones_f", [P, 32])
        bck = sb("bck", [P, GU, P])
        ones_k = sb("ones_k", [P, 32])
        amx = sb("amx", [P, TILES])
        amn = sb("amn", [P, TILES])
        E = sb("E", [P, 2, FA, GU * G])
        a_rep = sb("a_rep", [NA * KH, 2, U * FA, FB], bf16)
        a_diag = sb("a_diag", [P, 2, U * FA, KH, FB], bf16)
        q_st = sb("q_st", [P, 2, U, G], bf16)
        q_out = sb("q_out", [P, 2, 5, G], bf16)
        v_st = sb("v_st", [P, 2, U, FA, 32])
        rS = sb("rS", [P, G])
        zS = sb("zS", [P, 2, 2 * G])
        ks = sb("ks", [BT, 2, J])
        s0 = sb("s0", [P, 10, F])
        s0m = sb("s0m", [P, 2])
        arg0 = sb("arg0", [P, C0])
        w0 = sb("w0", [P, C0])
        y0 = sb("y0", [P, C0])
        y0T = sb("y0T", [P, NCH0, P])
        o0 = sb("o0", [P, J])
        qf = sb("qf", [P, 4, G])
        a0, q0, v0, m0, t0, sum0, rec0 = (s0[:, n, :] for n in range(7))

        bigf = big[:].rearrange("p c j -> p (c j)")
        NX = TILES * F
        a1 = bigf[:, 0:NX]
        a_hi = bigf[:, NX:NX + NX // 2].bitcast(bf16)
        a_md = bigf[:, NX + NX // 2:2 * NX].bitcast(bf16)
        a_lo = bigf[:, 2 * NX:2 * NX + NX // 2].bitcast(bf16)

        psA = pb("psA", [P, 3, 512])
        psS = pb("psS", [P, 512])
        psB = pb("psB", [P, 512])
        psZ = pb("psZ", [P, 512])
        psM = pb("psM", [P, 2, 512])

        loaded = sem("loaded")
        loaded_x = sem("loaded_x")
        loaded_cw1 = sem("loaded_cw1")
        prep = sem("prep")
        a_split = sem("a_split")
        a_stored = sem("a_stored")
        mask_ready = sem("mask_ready")
        diag_zeroed = sem("diag_zeroed")
        a_loaded = sem("a_loaded")
        a_built = sem("a_built")
        v_built = sem("v_built")
        q_split = sem("q_split")
        q_stored = sem("q_stored")
        q_loaded = sem("q_loaded")
        arg_done = sem("arg_done")
        exp_done = sem("exp_done")
        sum_done = sem("sum_done")
        recip_done = sem("recip_done")
        spread_done = sem("spread_done")
        norm_done = sem("norm_done")
        z_done = sem("z_done")
        z_copied = sem("z_copied")
        z_stored = [sem(f"z_stored{h}") for h in range(2)]
        ew_step = sem("ew_step")
        prod0 = sem("prod0")
        arg0_done = sem("arg0_done")
        exp0_done = sem("exp0_done")
        recip0_done = sem("recip0_done")
        w0_done = sem("w0_done")
        y0_done = sem("y0_done")
        misc_done = sem("misc_done")
        misc_used = sem("misc_used")
        q_chain = sem("q_chain")
        q_read = sem("q_read")
        ks_stored = sem("ks_stored")
        z_loaded = sem("z_loaded")
        f_tr = sem("f_tr")
        f_cp = sem("f_cp")
        f_mm = sem("f_mm")
        f_out = sem("f_out")
        out_stored = sem("out_stored")

        block = ctx.enter_context(nc.Block())
        NLOOP = (TILES - 4) // 2

        def tiles_of(engine, body):
            for t in range(2):
                body(t, t, True, True, True)
            with engine.Fori(1, NLOOP) as pair:
                for s in range(2):
                    body(pair * 2 + s, s, True, True, True)
            for t in range(2 * NLOOP, TILES):
                body(t, t % 2, t + EW_LEAD < TILES, t + SB_LEAD < TILES, t + 1 < TILES)

        N_CONST = 9

        @block.sync
        def _(sp):
            sp.dma_start(xr[:], x_rows).then_inc(loaded_x, 16)
            sp.dma_start(w_sb[:, 0:5, :], w_rows).then_inc(loaded_x, 16)
            for dst, src in ((ident[:], ident_d), (dga[:], diag_a), (ones_f[:], sum_f), (bck[:], bcast_k), (ones_k[:], sum_k),
                             (fbm[:], fb_mask), (wvu[:], wv_units)):
                sp.dma_start(dst, src).then_inc(loaded, 16)
            sp.dma_start(cw0_sb[0:CH0, 0:NCH0 - 1, :], cw0[0:CH0 * (NCH0 - 1)].rearrange("(c p) j -> p c j", p=CH0)).then_inc(loaded, 16)
            sp.dma_start(cw0_sb[0:C0 - CH0 * (NCH0 - 1), NCH0 - 1, :], cw0[CH0 * (NCH0 - 1):C0]).then_inc(loaded, 16)
            sp.wait_ge(a_split, 3)
            for n, part in enumerate((a_hi, a_md, a_lo)):
                sp.dma_start(a_parts[n], part).then_inc(a_stored, 16)
            sp.wait_ge(a_stored, 48)
            sp.dma_start(big[0:CH1], cw1.rearrange("(c p) j -> p c j", p=CH1)).then_inc(loaded_cw1, 16)

            def load_a(t, s, used=None):
                sp.dma_start(xu[:, s], x_units[:, bass.ds(t * U * FA, U * FA)]).then_inc(a_loaded, 16)
                for n, part in enumerate((0, 1, 2, 0, 1, 0)):
                    if n == 1 and used is not None:
                        sp.wait_ge(arg_done, used)
                    if n == 2 and used is not None:
                        sp.wait_ge(q_loaded, 128 * t)
                    if n == 3 and used is not None:
                        sp.wait_ge(ks_stored, 16 * (t - 1 + SB_LEAD))
                    src = a_parts[part, :, bass.ds(t * F, F)].rearrange("(u k) f -> k u f", k=KH)
                    sp.dma_start(a_rep[n * KH:(n + 1) * KH, s].rearrange("p (u a) b -> p u (a b)", u=U), src).then_inc(a_loaded, 16)

            def move_q(t, s):
                sp.wait_ge(q_split, t + 1)
                sp.dma_start(q_parts[s].rearrange("n p g -> p n g"), q_out[:, s]).then_inc(q_stored, 16)
                sp.wait_ge(q_stored, (t + 1) * 16)
                for n, part in enumerate((0, 0, 0, 1, 1, 2, 3, 4)):
                    src = q_parts[s, part].rearrange("(u k) g -> k u g", k=KH)
                    sp.dma_start(q_st[n * KH:(n + 1) * KH, s], src).then_inc(q_loaded, 16)

            load_a(0, 0)
            move_q(0, 0)
            

            def body(t, s, ew, sbk, nxt):
                if nxt:
                    sp.wait_ge(v_built, t)
                    load_a(t + 1, 1 - s, 2 * CHUNKS * t)
                    move_q(t + 1, 1 - s)
                if sbk:
                    sp.wait_ge(misc_used, 6 * (t + SB_LEAD + 1))
                    sp.dma_start(out[bass.ds((t + SB_LEAD) * BT, BT), 0:J], ks[:, s]).then_inc(ks_stored, 16)
                for h in range(2):
                    sp.wait_ge(z_copied, 2 * t + h + 1)
                    zd = z_dram[bass.ds(BT * t + 2 * h, 2)]
                    for fa in range(FA):
                        row = 32 * fa if fa < 4 else 96 + FB
                        sp.dma_start(zd[:, fa * FB:(fa + 1) * FB, :].rearrange("b f g -> f b g"),
                                     zS[row:row + FB, h].rearrange("f (b g) -> f b g", b=2)).then_inc(z_stored[h], 16)

            for t in range(SB_LEAD):
                sp.wait_ge(misc_used, 6 * (t + 1))
                if t:
                    sp.wait_ge(ks_stored, 16 * t)
                sp.dma_start(out[t * BT:(t + 1) * BT, 0:J], ks[:, t % 2]).then_inc(ks_stored, 16)
            tiles_of(sp, body)
            sp.wait_ge(ks_stored, 16 * TILES)
            for h in range(2):
                sp.wait_ge(z_stored[h], 16 * FA * TILES)
            zb = E[:].rearrange("p s a g -> p (s a g)")
            for n in range(B // P):
                if n:
                    sp.wait_ge(f_tr, n * NCH1 // 4)
                sp.dma_start(zb, z_dram[n * P:(n + 1) * P].rearrange("b f g -> b (f g)")).then_inc(z_loaded, 16)
            for n in range(B // P):
                sp.wait_ge(f_out, n + 1)
                sp.dma_start(out[n * P:(n + 1) * P, J:2 * J], w0[:, n * J:(n + 1) * J]).then_inc(out_stored, 16)
            sp.wait_ge(out_stored, 16 * (B // P))

        @block.tensor
        def _(pe):
            def arg_chunk(n, c, hs, s):
                fa, p = divmod(c, 2)
                bank = ARG_BANK[c]
                if not (isinstance(n, int) and n == 0 and c < 3):
                    pe.wait_ge(exp_done, n * CHUNKS + c - ARG_BACK[c] + 1)
                for j in range(2):
                    u = GU * hs + 2 * p + j
                    mm = nc.tensor.matmul(psA[:, bank, j * G:(j + 1) * G], a_diag[:, s, u * FA + fa].rearrange("p k b -> p (k b)"),
                                          q_st[:, s, u, :], start=True, stop=True)
                mm.then_inc(arg_done, 1)

            def group_ready(n, t, hs):
                if hs == 0:
                    pe.wait_ge(q_loaded, 16 * 8 * (t + 1))
                    pe.wait_ge(a_built, t + 1)

            def sums(i, e):
                pe.wait_ge(exp_done, (i + 1) * CHUNKS)
                pe.wait_ge(recip_done, i)
                for fa in range(FA):
                    for u in range(GU):
                        mm = nc.tensor.matmul(psS[32 * u:32 * u + 32, 0:G], ones_f[:], E[:, e, fa, u * G:(u + 1) * G],
                                              start=fa == 0, stop=fa == FA - 1)
                mm.then_inc(sum_done, 1)

            def spread(i, p):
                pe.wait_ge(recip_done, i + 1)
                pe.wait_ge(norm_done, 2 * i + p)
                for j in range(2):
                    mm = nc.tensor.matmul(psB[:, j * G:(j + 1) * G], bck[:, 2 * p + j, :], rS[:], start=True, stop=True)
                mm.then_inc(spread_done, 1)

            def ksum(i, b, h, s, e):
                pe.wait_ge(norm_done, 2 * i + b + 1)
                if b == 0:
                    pe.wait_ge(z_copied, i)
                for kh in range(2):
                    u = 2 * b + kh
                    for fa in range(FA):
                        q = min(fa, 3)
                        mm = nc.tensor.matmul(psZ[32 * q:32 * q + 32, b * G:(b + 1) * G], v_st[:, s, GU * h + u, fa, :],
                                              E[:, e, fa, u * G:(u + 1) * G],
                                              start=kh == 0 and fa < 4, stop=kh == 1 and fa != 3)
                if b == 1:
                    mm.then_inc(z_done, 1)

            def misc_free(T, j):
                if not (isinstance(T, int) and 6 * T + j < 2):
                    pe.wait_ge(misc_used, 6 * T + j - 1)

            def l0_transpose(T, j):
                if j == 0:
                    pe.wait_ge(y0_done, T + 1)
                misc_free(T, j)
                for c in range(4 * j, min(4 * j + 4, NCH0)):
                    n = min(CH0, C0 - c * CH0)
                    mm = nc.tensor.transpose(psM[0:n, j % 2, (c % 4) * P:(c % 4 + 1) * P], y0[:, c * CH0:c * CH0 + n], ident[:])
                mm.then_inc(misc_done, 1)

            def l0_product(T, c0, c1):
                if c0 == 0:
                    misc_free(T, 4)
                pe.wait_ge(misc_used, 6 * T + min((c1 - 1) // 4, 3) + 1)
                for c in range(c0, c1):
                    n = min(CH0, C0 - c * CH0)
                    mm = nc.tensor.matmul(psM[:, 0, 0:J], y0T[0:n, c, :], cw0_sb[0:n, c, :], start=c == 0, stop=c == NCH0 - 1)
                if c1 == NCH0:
                    mm.then_inc(misc_done, 1)

            def l0_ksum(T):
                misc_free(T, 5)
                pe.wait_ge(misc_used, 6 * T + 5)
                nc.tensor.matmul(psM[0:32, 1, 0:J], ones_k[:], o0[:], start=True, stop=True).then_inc(misc_done, 1)

            def body(t, s, ew, sbk, nxt):
                T = t + SB_LEAD
                for h in range(2):
                    i, e = 2 * t + h, h
                    args = nxt or h == 0
                    nh, ns = 1 - h, s if h == 0 else 1 - s
                    if args:
                        group_ready(i + 1, t + 1, nh)
                        for c in (0, 1):
                            arg_chunk(i + 1, c, nh, ns)
                    sums(i, e)
                    if args:
                        for c in (2, 3):
                            arg_chunk(i + 1, c, nh, ns)
                    if sbk and h == 0:
                        l0_transpose(T, 0)
                        l0_transpose(T, 1)
                    if sbk and h == 1:
                        l0_product(T, 6, NCH0)
                    spread(i, 0)
                    if args:
                        for c in (4, 5):
                            arg_chunk(i + 1, c, nh, ns)
                    if sbk and h == 0:
                        l0_transpose(T, 2)
                        l0_transpose(T, 3)
                    if sbk and h == 1:
                        l0_ksum(T)
                    if args:
                        for c in (6, 7):
                            arg_chunk(i + 1, c, nh, ns)
                    spread(i, 1)
                    ksum(i, 0, h, s, e)
                    if args:
                        for c in (8, 9):
                            arg_chunk(i + 1, c, nh, ns)
                    if sbk and h == 0:
                        l0_product(T, 0, 6)
                    ksum(i, 1, h, s, e)

            pe.wait_ge(loaded, 16 * N_CONST)
            for T in range(SB_LEAD):
                for j in range(4):
                    l0_transpose(T, j)
                l0_product(T, 0, NCH0)
                l0_ksum(T)
            group_ready(0, 0, 0)
            pe.wait_ge(diag_zeroed, 1)
            pe.wait_ge(v_built, 1)
            for c in range(CHUNKS):
                arg_chunk(0, c, 0, 0)

            def body_v(t, s, ew, sbk, nxt):
                if nxt:
                    pe.wait_ge(v_built, t + 1)
                else:
                    pe.wait_ge(v_built, TILES)
                body(t, s, ew, sbk, nxt)

            tiles_of(pe, body_v)

            zb = E[:].rearrange("p s a g -> p (s a g)")
            pe.wait_ge(loaded_cw1, 16)
            for n in range(B // P):
                pe.wait_ge(z_loaded, 16 * (n + 1))

                def product(r):
                    pe.wait_ge(f_cp, n * NCH1 // 4 + r + 1)
                    for c in range(4 * r, 4 * r + 4):
                        mm = nc.tensor.matmul(psZ[:, 0:J], y0T[0:CH1, (c % 8), :], big[0:CH1, c, :], start=c == 0, stop=c == NCH1 - 1)
                    mm.then_inc(f_mm, 1)

                for r in range(NCH1 // 4):
                    m = n * NCH1 // 4 + r
                    if m >= 2:
                        pe.wait_ge(f_cp, m - 1)
                    for c in range(4 * r, 4 * r + 4):
                        mm = nc.tensor.transpose(psM[0:CH1, r % 2, (c % 4) * P:(c % 4 + 1) * P], zb[:, c * CH1:(c + 1) * CH1], ident[:])
                    mm.then_inc(f_tr, 1)
                    if r == 0 and n:
                        pe.wait_ge(f_out, n)
                    if r:
                        product(r - 1)
                product(NCH1 // 4 - 1)

        @block.scalar
        def _(act):
            def exps(n, e, cs):
                for c in cs:
                    act.wait_ge(arg_done, n * CHUNKS + c + 1)
                    if c == 0 and not (isinstance(n, int) and n < 2):
                        act.wait_ge(z_done, n - 1)
                    nc.scalar.activation(E[:, e, c // 2, (c % 2) * 2 * G:(c % 2 + 1) * 2 * G], psA[:, ARG_BANK[c], 0:2 * G],
                                         ACT.Exp).then_inc(exp_done, 1)

            def exp0(T):
                act.wait_ge(arg0_done, T + 1)
                nc.scalar.activation(arg0[:], arg0[:], ACT.Exp).then_inc(exp0_done, 1)

            def chunk_copy(T, j):
                act.wait_ge(misc_done, 6 * T + j + 1)
                if j == 3:
                    nc.scalar.copy(y0T[0:C0 - CH0 * 12, 12, :], psM[0:C0 - CH0 * 12, 1, 0:P]).then_inc(misc_used, 1)
                else:
                    nc.scalar.copy(y0T[0:CH0, 4 * j:4 * j + 4, :].rearrange("p c n -> p (c n)"), psM[0:CH0, j % 2, :]).then_inc(misc_used, 1)

            def out_copy(T):
                act.wait_ge(misc_done, 6 * T + 5)
                if not (isinstance(T, int) and T == 0):
                    act.wait_ge(q_read, T)
                nc.scalar.copy(o0[:], psM[:, 0, 0:J]).then_inc(misc_used, 1)

            def ks_copy(T, s):
                act.wait_ge(misc_done, 6 * T + 6)
                if not (isinstance(T, int) and T < 2):
                    act.wait_ge(ks_stored, 16 * (T - 1))
                nc.scalar.copy(ks[:, s], psM[0:BT, 1, 0:J]).then_inc(misc_used, 1)

            def z_copy(t, h):
                act.wait_ge(z_done, 2 * t + h + 1)
                act.wait_ge(z_stored[h], 16 * FA * t)
                nc.scalar.copy(zS[:, h], psZ[:, 0:2 * G]).then_inc(z_copied, 1)

            def body(t, s, ew, sbk, nxt):
                T = t + SB_LEAD
                for h in range(2):
                    i = 2 * t + h
                    args = nxt or h == 0
                    e = 1 - h
                    if args:
                        exps(i + 1, e, (0, 1))
                    if args:
                        exps(i + 1, e, (2, 3))
                    if sbk and h == 0:
                        chunk_copy(T, 0)
                        chunk_copy(T, 1)
                    if sbk and h == 1:
                        out_copy(T)
                    if args:
                        exps(i + 1, e, (4, 5))
                    if sbk and h == 0:
                        chunk_copy(T, 2)
                        chunk_copy(T, 3)
                    if ew and h == 1:
                        exp0(t + EW_LEAD)
                    if sbk and h == 1:
                        ks_copy(T, s)
                    if args:
                        exps(i + 1, e, (6, 7))
                    if args:
                        exps(i + 1, e, (8, 9))
                    z_copy(t, h)

            for T in range(EW_LEAD):
                exp0(T)
                if T:
                    for j in range(4):
                        chunk_copy(T - 1, j)
                    out_copy(T - 1)
                    ks_copy(T - 1, T - 1)
            exps(0, 0, range(CHUNKS))
            tiles_of(act, body)
            for m in range(B // P * NCH1 // 4):
                act.wait_ge(f_tr, m + 1)
                if m >= 2:
                    act.wait_ge(f_mm, m - 1)
                nc.scalar.copy(y0T[0:CH1, 4 * (m % 2):4 * (m % 2) + 4, :].rearrange("p c n -> p (c n)"),
                               psM[0:CH1, m % 2, :]).then_inc(f_cp, 1)

        @block.gpsimd
        def _(pool):
            pool.wait_ge(loaded, 16 * N_CONST)
            nc.gpsimd.memset(v_st[:], 0.0).then_inc(mask_ready, 1)
            for kh in range(2):
                nc.gpsimd.tensor_tensor(wv_mask[:, kh], wvu[:, kh].unsqueeze(2).to_broadcast((P, FA, FB)),
                                        fbm[:].unsqueeze(1).to_broadcast((P, FA, FB)), ALU.mult).then_inc(mask_ready, 1)
            for s in range(2):
                pool.wait_ge(mask_ready, 3 + s)
                nc.gpsimd.tensor_copy(a_diag[NA * KH:P, s], dga[NA * KH:P].unsqueeze(1).unsqueeze(3).to_broadcast(
                    (2 * KH, U * FA, KH, FB))).then_inc(mask_ready, 1)
            pool.wait_ge(mask_ready, 5)
            nc.gpsimd.sem_inc(diag_zeroed, 1)

            def build(t, s):
                pool.wait_ge(a_loaded, 16 * (NA + 1) * (t + 1))
                if not (isinstance(t, int) and t < 2):
                    pool.wait_ge(arg_done, 2 * CHUNKS * (t - 1))
                nc.gpsimd.tensor_tensor(a_diag[0:NA * KH, s],
                                        a_rep[:, s].unsqueeze(2).to_broadcast((NA * KH, U * FA, KH, FB)),
                                        dga[0:NA * KH].unsqueeze(1).unsqueeze(3).to_broadcast((NA * KH, U * FA, KH, FB)),
                                        ALU.mult).then_inc(a_built, 1)
                if not (isinstance(t, int) and t < 2):
                    pool.wait_ge(z_done, 2 * (t - 1))
                xt = xu[:, s].rearrange("p (b h a) -> p h b a", h=2, a=FA)
                vt = v_st[:, s].rearrange("p (b h) a c -> p h b a c", h=2)
                for kh in range(2):
                    for lo, hi, col in ((0, 4, 0), (4, 5, FB)):
                        last = nc.gpsimd.tensor_tensor(vt[:, kh, :, lo:hi, col:col + FB],
                                                       xt[:, kh, :, lo:hi].unsqueeze(3).to_broadcast((P, U // 2, hi - lo, FB)),
                                                       wv_mask[:, kh, lo:hi].unsqueeze(1).to_broadcast((P, U // 2, hi - lo, FB)), ALU.mult)
                last.then_inc(v_built, 1)

            def product0(T):
                pool.wait_ge(ew_step, EW_STEPS * T + 3)
                if not (isinstance(T, int) and T == 0):
                    pool.wait_ge(y0_done, T)
                nc.gpsimd.tensor_tensor(arg0[:].rearrange("p (f g) -> p f g", f=F), a0.unsqueeze(2).to_broadcast((P, F, F)),
                                        q0.unsqueeze(1).to_broadcast((P, F, F)), ALU.mult).then_inc(prod0, 1)

            def weights0(T):
                pool.wait_ge(recip0_done, T + 1)
                nc.gpsimd.tensor_tensor(w0[:].rearrange("p (f g) -> p f g", f=F), v0.unsqueeze(2).to_broadcast((P, F, F)),
                                        rec0.unsqueeze(1).to_broadcast((P, F, F)), ALU.mult).then_inc(w0_done, 1)

            for T in range(EW_LEAD):
                product0(T)
                weights0(T)
            build(0, 0)

            def body(t, s, ew, sbk, nxt):
                if ew:
                    product0(t + EW_LEAD)
                if nxt:
                    build(t + 1, 1 - s)
                if ew:
                    weights0(t + EW_LEAD)

            tiles_of(pool, body)

        @block.vector
        def _(dve):
            def w(n, width):
                return w_sb[:, n, 0:width]

            dve.wait_ge(loaded_x, 32)
            x3 = xr[:].rearrange("p (t f) -> p t f", f=F)
            a3 = a1.rearrange("p (t f) -> p t f", f=F)
            v = nc.vector
            v.tensor_tensor(a3, x3, w(3, F).unsqueeze(1).to_broadcast((P, TILES, F)), ALU.mult).then_inc(prep, 1)
            dve.wait_ge(prep, 1)
            v.tensor_reduce(amx[:], a3, AX.X, ALU.max).then_inc(prep, 1)
            v.tensor_reduce(amn[:], a3, AX.X, ALU.min).then_inc(prep, 1)
            v.tensor_copy(a_hi, a1).then_inc(a_split, 1)
            dve.wait_ge(a_split, 1)
            v.tensor_tensor(a1, a1, a_hi, ALU.subtract).then_inc(prep, 1)
            dve.wait_ge(prep, 4)
            v.tensor_copy(a_md, a1).then_inc(a_split, 1)
            dve.wait_ge(a_split, 2)
            v.tensor_tensor(a1, a1, a_md, ALU.subtract).then_inc(prep, 1)
            dve.wait_ge(prep, 5)
            v.tensor_copy(a_lo, a1).then_inc(a_split, 1)

            def ew_small(T):
                if not (isinstance(T, int) and T == 0):
                    dve.wait_ge(y0_done, T)
                    dve.wait_ge(w0_done, T)
                x = xr[:, bass.ds(T * F, F)]
                v.tensor_tensor(a0, x, w(1, F), ALU.mult).then_inc(ew_step, 1)
                v.tensor_tensor(q0, x, w(0, F), ALU.mult).then_inc(ew_step, 1)
                v.tensor_tensor(v0, x, w(2, F), ALU.mult).then_inc(ew_step, 1)
                dve.wait_ge(ew_step, EW_STEPS * T + 3)
                v.tensor_reduce(s0m[:, 0:1], a0, AX.X, ALU.max).then_inc(ew_step, 1)
                v.tensor_reduce(s0m[:, 1:2], a0, AX.X, ALU.min).then_inc(ew_step, 1)
                dve.wait_ge(ew_step, EW_STEPS * T + 5)
                v.tensor_scalar(t0, q0, s0m[:, 0:1], None, ALU.mult).then_inc(ew_step, 1)
                dve.wait_ge(ew_step, EW_STEPS * T + 6)
                v.scalar_tensor_tensor(out=m0, in0=q0, scalar=s0m[:, 1:2], in1=t0, op0=ALU.mult, op1=ALU.max).then_inc(ew_step, 1)

            def ew_shift(T):
                dve.wait_ge(ew_step, EW_STEPS * T + 7)
                dve.wait_ge(prod0, T + 1)
                p3 = arg0[:].rearrange("p (f g) -> p f g", f=F)
                v.tensor_tensor(p3, p3, m0.unsqueeze(1).to_broadcast((P, F, F)), ALU.subtract).then_inc(arg0_done, 1)

            def ew_sum(T):
                dve.wait_ge(exp0_done, T + 1)
                v.tensor_reduce(sum0, arg0[:].rearrange("p (f g) -> p g f", f=F), AX.X, ALU.add).then_inc(ew_step, 1)
                dve.wait_ge(ew_step, EW_STEPS * T + 8)
                v.reciprocal(rec0, sum0).then_inc(recip0_done, 1)

            def ew_apply(T):
                dve.wait_ge(w0_done, T + 1)
                if not (isinstance(T, int) and T == 0):
                    dve.wait_ge(misc_done, 6 * T - 2)
                v.tensor_tensor(y0[:], arg0[:], w0[:], ALU.mult).then_inc(y0_done, 1)

            def q_parts_of(T, s):
                dve.wait_ge(misc_used, 6 * T + 6)
                if not (isinstance(T, int) and T < 2):
                    dve.wait_ge(q_stored, 16 * (T - 1))
                q, m, r, r2 = (qf[:, n, :] for n in range(4))
                at = Q_STEPS * T
                v.tensor_tensor(q, o0[:], w(4, G), ALU.mult).then_inc(q_chain, 1)
                dve.wait_ge(q_chain, at + 1)
                v.tensor_scalar(m, q, amx[:, bass.ds(T, 1)], None, ALU.mult).then_inc(q_chain, 1)
                v.tensor_copy(q_out[:, s, 0, :], q).then_inc(q_chain, 1)
                dve.wait_ge(q_chain, at + 3)
                v.scalar_tensor_tensor(out=m, in0=q, scalar=amn[:, bass.ds(T, 1)], in1=m, op0=ALU.mult, op1=ALU.max).then_inc(q_chain, 1)
                v.tensor_tensor(r, q, q_out[:, s, 0, :], ALU.subtract).then_inc(q_chain, 1)
                dve.wait_ge(q_chain, at + 5)
                v.tensor_copy(q_out[:, s, 3, :], m).then_inc(q_chain, 1)
                v.tensor_copy(q_out[:, s, 1, :], r).then_inc(q_chain, 1)
                dve.wait_ge(q_chain, at + 7)
                v.tensor_tensor(r2, m, q_out[:, s, 3, :], ALU.subtract).then_inc(q_chain, 1)
                v.tensor_tensor(r, r, q_out[:, s, 1, :], ALU.subtract).then_inc(q_chain, 1)
                dve.wait_ge(q_chain, at + 9)
                v.tensor_copy(q_out[:, s, 4, :], r2).then_inc(q_chain, 1)
                v.tensor_copy(q_out[:, s, 2, :], r).then_inc(q_chain, 1)
                dve.wait_ge(q_chain, at + 11)
                dve.sem_inc(q_split, 1)
                dve.sem_inc(q_read, 1)

            def recip(i):
                dve.wait_ge(sum_done, i + 1)
                dve.wait_ge(spread_done, 2 * i)
                v.reciprocal(rS[:], psS[:, 0:G]).then_inc(recip_done, 1)

            def normalise(i, p, e):
                dve.wait_ge(spread_done, 2 * i + p + 1)
                x = E[:, e, :, p * 2 * G:(p + 1) * 2 * G]
                v.tensor_tensor(x, x, psB[:, 0:2 * G].unsqueeze(1).to_broadcast((P, FA, 2 * G)), ALU.mult).then_inc(norm_done, 1)

            def body(t, s, ew, sbk, nxt):
                X, Q = t + EW_LEAD, t + SB_LEAD
                i = 2 * t
                if ew:
                    ew_small(X)
                recip(i)
                normalise(i, 0, 0)
                if ew:
                    ew_shift(X)
                normalise(i, 1, 0)
                recip(i + 1)
                normalise(i + 1, 0, 1)
                if ew:
                    ew_sum(X)
                normalise(i + 1, 1, 1)
                if sbk:
                    q_parts_of(Q, s)
                if ew:
                    ew_apply(X)

            for T in range(EW_LEAD):
                ew_small(T)
                ew_shift(T)
                ew_sum(T)
                ew_apply(T)
                if T:
                    q_parts_of(T - 1, T - 1)
            tiles_of(dve, body)
            for n in range(B // P):
                dve.wait_ge(f_mm, (n + 1) * NCH1 // 4)
                v.tensor_copy(w0[:, n * J:(n + 1) * J], psZ[:, 0:J]).then_inc(f_out, 1)


def kernel(r_inputs, L0_rec_wq0, L0_rec_wk0, L0_rec_wv0, L0_rec_cw0, L0_rec_wq1, L0_rec_wk1, L0_rec_wv1, L0_rec_cw1):
    import numpy as np
    import ml_dtypes
    import concourse.bacc as bacc
    from concourse.bass_utils import run_bass_kernel_spmd

    x = np.asarray(r_inputs)
    c = np.ascontiguousarray
    rows = x.transpose(0, 2, 1).reshape(TILES, P, F)
    x_rows = c(rows.transpose(1, 0, 2).reshape(P, TILES * F))
    x_units = c(x.reshape(TILES, BT, FA, FB, 2, KH).transpose(5, 3, 0, 1, 4, 2).reshape(P, TILES * U * FA))
    w_rows = np.zeros((P, 5, G), np.float32)
    for n, wt in enumerate((L0_rec_wq0, L0_rec_wk0, L0_rec_wv0, L0_rec_wk1, L0_rec_wq1)):
        wt = np.asarray(wt)[0].T
        w_rows[:, n, :wt.shape[1]] = np.tile(wt, (BT, 1))
    wv_units = c(np.asarray(L0_rec_wv1)[0].reshape(FA, FB, 2, KH).transpose(3, 1, 2, 0).reshape(P, 2, FA))
    p = np.arange(P)
    ident = np.eye(P, dtype=np.float32)
    diag_a = (p[:, None] % KH == np.arange(KH)).astype(np.float32)
    diag_a[NA * KH:] *= -1
    sum_f = (p[:, None] // FB == np.arange(32) % KH).astype(np.float32)
    bcast_k = np.zeros((P, GU, P), np.float32)
    for u in range(GU):
        bcast_k[32 * u + p // FB, u, p] = 1
    sum_k = (p[:, None] // K == np.arange(32)).astype(np.float32)
    fb_mask = (p[:, None] % FB == np.arange(FB)).astype(np.float32)
    arrays = {
        "x_rows": x_rows, "x_units": x_units, "w_rows": w_rows, "wv_units": wv_units,
        "cw0": c(np.asarray(L0_rec_cw0)[0]), "cw1": c(np.asarray(L0_rec_cw1)[0]),
        "ident_d": ident, "diag_a": diag_a.astype(ml_dtypes.bfloat16), "sum_f": sum_f, "bcast_k": bcast_k,
        "sum_k": sum_k, "fb_mask": fb_mask,
    }
    nc = bacc.Bacc("TRN2", target_bir_lowering=False, num_devices=1)
    args = {n: nc.dram_tensor(n, a.shape, mybir.dt.from_np(a.dtype), kind="ExternalInput").ap() for n, a in arrays.items()}
    out = nc.dram_tensor("out", (B, 2 * J), mybir.dt.float32, kind="ExternalOutput").ap()
    cin_kernel(nc, *args_in_order(args), out)
    r = run_bass_kernel_spmd(nc, [arrays], core_ids=[0])
    return r.results[0]["out"]


def args_in_order(args):
    return [args[n] for n in ("x_rows", "x_units", "w_rows", "wv_units", "cw0", "cw1", "ident_d", "diag_a", "sum_f",
                              "bcast_k", "sum_k", "fb_mask")]
```

```python
import concourse.bass as bass
from concourse import mybir
from contextlib import ExitStack

B, F, K, J = 512, 40, 32, 200
G = J
P = 128
TILES = B * K // P
BT = P // K
KH = 16
U = P // KH
FA, FB = 5, 8
GU = 4
NA = 6
C0 = F * F
CH0 = 124
NCH0 = -(-C0 // CH0)
C1, CH1 = F * G, 125
NCH1 = C1 // CH1
CHUNKS = FA * 2
ARG_BANK = [0, 1, 2, 0, 1, 2, 0, 1, 2, 1]
ARG_BACK = [4, 2, 4, 3, 3, 3, 3, 3, 3, 2]
A_LEAD, EW_LEAD, SB_LEAD = 4, 3, 2
EW_STEPS, Q_STEPS = 7, 11


def cin_kernel(nc, x_rows, x_units, w_rows, wv_units, cw0, cw1, ident_d, diag_a, sum_f, bcast_k, sum_k, fb_mask, out):
    f32, bf16 = mybir.dt.float32, mybir.dt.bfloat16
    ALU, ACT, AX = mybir.AluOpType, mybir.ActivationFunctionType, mybir.AxisListType

    with ExitStack() as ctx:
        def sb(name, shape, dt=f32):
            return ctx.enter_context(nc.sbuf_tensor(name, shape, dt))

        def pb(name, shape):
            return ctx.enter_context(nc.psum_tensor(name, shape, f32))

        def sem(name):
            return ctx.enter_context(nc.semaphore(name))

        a_parts = nc.dram_tensor("a_parts", (3, P, TILES * F), bf16, kind="Internal").ap()
        q_parts = nc.dram_tensor("q_parts", (2, 5, P, G), bf16, kind="Internal").ap()
        z_dram = nc.dram_tensor("z_dram", (B, F, G), f32, kind="Internal").ap()

        xt0 = sb("xt0", [P, F])
        xu = sb("xu", [P, 2, U * FA])
        w_sb = sb("w_sb", [P, 5, G])
        wvu = sb("wvu", [P, 2, FA])
        wv_mask = sb("wv_mask", [P, 2, FA, FB])
        fbm = sb("fbm", [P, FB])
        cw0_sb = sb("cw0_sb", [P, NCH0, J])
        big = sb("big", [P, NCH1, J])
        ident = sb("ident", [P, P])
        dga = sb("dga", [P, KH], bf16)
        ones_f = sb("ones_f", [P, 32])
        bck = sb("bck", [P, GU, P])
        ones_k = sb("ones_k", [P, 32])
        amx = sb("amx", [P, TILES])
        amn = sb("amn", [P, TILES])
        E = sb("E", [P, 4, FA, GU * G])
        a_rep = sb("a_rep", [NA * KH, 2, U * FA, FB], bf16)
        a_diag = sb("a_diag", [P, 2, U * FA, KH, FB], bf16)
        q_st = sb("q_st", [P, 2, U, G], bf16)
        q_out = sb("q_out", [P, 2, 5, G], bf16)
        v_st = sb("v_st", [P, 2, U, FA, 32])
        rS = sb("rS", [P, G])
        zS = sb("zS", [P, 2, 2 * G])
        ks = sb("ks", [BT, J])
        s0 = sb("s0", [P, 2, 6, F])
        s0m = sb("s0m", [P, 2])
        arg0 = sb("arg0", [P, 2, C0])
        w0 = sb("w0", [P, C0])
        y0T = sb("y0T", [P, NCH0, P])
        o0 = sb("o0", [P, J])
        qf = sb("qf", [P, 3, G])

        bigf = big[:].rearrange("p c j -> p (c j)")
        NX = TILES * F
        a1 = bigf[:, 0:NX]
        xr = E[:].rearrange("p s a g -> p (s a g)")[:, 0:NX]
        a_hi = bigf[:, NX:NX + NX // 2].bitcast(bf16)
        a_md = bigf[:, NX + NX // 2:2 * NX].bitcast(bf16)
        a_lo = bigf[:, 2 * NX:2 * NX + NX // 2].bitcast(bf16)

        psA = pb("psA", [P, 3, 512])
        psS = pb("psS", [P, 512])
        psB = pb("psB", [P, 512])
        psZ = pb("psZ", [P, 512])
        psM = pb("psM", [P, 2, 512])

        loaded = sem("loaded")
        loaded_x = sem("loaded_x")
        loaded_x0 = sem("loaded_x0")
        loaded_w = sem("loaded_w")
        loaded_cw1 = sem("loaded_cw1")
        prep = sem("prep")
        a_split = sem("a_split")
        a_stored = sem("a_stored")
        mask_ready = sem("mask_ready")
        diag_zeroed = sem("diag_zeroed")
        a_loaded = sem("a_loaded")
        a_built = sem("a_built")
        v_built = sem("v_built")
        q_split = sem("q_split")
        q_stored = sem("q_stored")
        q_loaded = sem("q_loaded")
        arg_done = sem("arg_done")
        exp_done = sem("exp_done")
        sum_done = sem("sum_done")
        recip_done = sem("recip_done")
        spread_done = sem("spread_done")
        norm_done = sem("norm_done")
        z_done = sem("z_done")
        z_copied = sem("z_copied")
        z_stored = [sem(f"z_stored{h}") for h in range(2)]
        ew_step = sem("ew_step")
        prod0 = sem("prod0")
        sum0_done = sem("sum0_done")
        arg0_done = sem("arg0_done")
        exp0_done = sem("exp0_done")
        recip0_done = sem("recip0_done")
        w0_done = sem("w0_done")
        y0_done = sem("y0_done")
        misc_done = sem("misc_done")
        misc_used = sem("misc_used")
        q_chain = sem("q_chain")
        q_read = sem("q_read")
        ks_stored = sem("ks_stored")
        z_loaded = [sem(f"z_loaded{n}") for n in range(2)]
        f_tr = sem("f_tr")
        f_cp = sem("f_cp")
        f_mm = sem("f_mm")
        f_out = sem("f_out")
        out_stored = sem("out_stored")

        block = ctx.enter_context(nc.Block())
        NLOOP = (TILES - 6) // 2

        def tiles_of(engine, body):
            for t in range(2):
                body(t, t, True, True, True, True, True)
            with engine.Fori(1, NLOOP) as pair:
                for s in range(2):
                    body(pair * 2 + s, s, True, True, True, True, True)
            for t in range(2 * NLOOP, TILES):
                body(t, t % 2, t + A_LEAD < TILES, t + EW_LEAD < TILES, t + SB_LEAD < TILES, t + 2 < TILES, t + 1 < TILES)

        N_CONST = 9

        @block.sync
        def _(sp):
            sp.dma_start(xt0[:], x_rows[:, 0:F]).then_inc(loaded_x0, 16)
            sp.dma_start(w_sb[:], w_rows).then_inc(loaded_w, 16)
            sp.dma_start(xr, x_rows).then_inc(loaded_x, 16)
            for dst, src in ((ident[:], ident_d), (dga[:], diag_a), (ones_f[:], sum_f), (bck[:], bcast_k), (ones_k[:], sum_k),
                             (fbm[:], fb_mask), (wvu[:], wv_units)):
                sp.dma_start(dst, src).then_inc(loaded, 16)
            sp.dma_start(cw0_sb[0:CH0, 0:NCH0 - 1, :], cw0[0:CH0 * (NCH0 - 1)].rearrange("(c p) j -> p c j", p=CH0)).then_inc(loaded, 16)
            sp.dma_start(cw0_sb[0:C0 - CH0 * (NCH0 - 1), NCH0 - 1, :], cw0[CH0 * (NCH0 - 1):C0]).then_inc(loaded, 16)
            sp.wait_ge(a_split, 3)
            for n, part in enumerate((a_hi, a_md, a_lo)):
                sp.dma_start(a_parts[n], part).then_inc(a_stored, 16)
            sp.wait_ge(a_stored, 48)
            sp.dma_start(big[0:CH1], cw1.rearrange("(c p) j -> p c j", p=CH1)).then_inc(loaded_cw1, 16)

            def load_a(t, s, t_now=None):
                sp.dma_start(xu[:, s], x_units[:, bass.ds(t * U * FA, U * FA)]).then_inc(a_loaded, 16)
                for n, part in enumerate((0, 1, 2, 0, 1, 0)):
                    if n == 3 and t_now is not None:
                        sp.wait_ge(ks_stored, 16 * (t_now + 1))
                    src = a_parts[part, :, bass.ds(t * F, F)].rearrange("(u k) f -> k u f", k=KH)
                    sp.dma_start(a_rep[n * KH:(n + 1) * KH, s].rearrange("p (u a) b -> p u (a b)", u=U), src).then_inc(a_loaded, 16)

            def move_q(t, s):
                sp.wait_ge(q_split, t + 1)
                sp.dma_start(q_parts[s].rearrange("n p g -> p n g"), q_out[:, s]).then_inc(q_stored, 16)
                sp.wait_ge(q_stored, (t + 1) * 16)
                for n, part in enumerate((0, 0, 0, 1, 1, 2, 3, 4)):
                    src = q_parts[s, part].rearrange("(u k) g -> k u g", k=KH)
                    sp.dma_start(q_st[n * KH:(n + 1) * KH, s], src).then_inc(q_loaded, 16)

            def load_x0(T):
                sp.dma_start(xt0[:], x_rows[:, bass.ds(T * F, F)]).then_inc(loaded_x0, 16)

            load_a(0, 0)
            for T in range(1, A_LEAD + 1):
                if T == A_LEAD:
                    for n in range(SB_LEAD):
                        sp.wait_ge(misc_used, 6 * (n + 1))
                        sp.dma_start(out[n * BT:(n + 1) * BT, 0:J], ks[:]).then_inc(ks_stored, 16)
                        if n == 0:
                            move_q(0, 0)
                            sp.wait_ge(ks_stored, 16)
                sp.wait_ge(ew_step, EW_STEPS * (T - 1) + 3)
                load_x0(T)
            sp.wait_ge(a_built, 1)
            load_a(1, 1)

            def body(t, s, eA, eB, sbk, nx2, nxt):
                if nxt:
                    move_q(t + 1, 1 - s)
                if not (isinstance(t, int) and t == 0):
                    store_z(2 * t - 1, 0)
                if eA and not (isinstance(t, int) and t + A_LEAD + 1 >= TILES):
                    sp.wait_ge(ew_step, EW_STEPS * (t + A_LEAD) + 3)
                    load_x0(t + A_LEAD + 1)
                if nx2:
                    sp.wait_ge(a_built, t + 2)
                    load_a(t + 2, s, t)
                store_z(2 * t, 1)
                if sbk:
                    if not nx2:
                        sp.wait_ge(ks_stored, 16 * (t + 1))
                    sp.wait_ge(misc_used, 6 * (t + SB_LEAD + 1))
                    sp.dma_start(out[bass.ds((t + SB_LEAD) * BT, BT), 0:J], ks[:]).then_inc(ks_stored, 16)

            def store_z(i, h):
                sp.wait_ge(z_copied, i + 1)
                zd = z_dram[bass.ds(2 * i, 2)]
                for fa in range(FA):
                    row = 32 * fa if fa < 4 else 96 + FB
                    sp.dma_start(zd[:, fa * FB:(fa + 1) * FB, :].rearrange("b f g -> f b g"),
                                 zS[row:row + FB, h].rearrange("f (b g) -> f b g", b=2)).then_inc(z_stored[h], 16)

            tiles_of(sp, body)
            store_z(2 * TILES - 1, 0)
            sp.wait_ge(ks_stored, 16 * TILES)
            for h in range(2):
                sp.wait_ge(z_stored[h], 16 * FA * TILES)
            zb = E[:].rearrange("p (n s) a g -> p n (s a g)", n=2)
            for n in range(B // P):
                if n > 1:
                    sp.wait_ge(f_tr, (n - 1) * NCH1 // 4)
                sp.dma_start(zb[:, n % 2], z_dram[n * P:(n + 1) * P].rearrange("b f g -> b (f g)")).then_inc(z_loaded[n % 2], 16)
            for n in range(B // P):
                sp.wait_ge(f_out, n + 1)
                sp.dma_start(out[n * P:(n + 1) * P, J:2 * J], w0[:, n * J:(n + 1) * J]).then_inc(out_stored, 16)
            sp.wait_ge(out_stored, 16 * (B // P))

        @block.tensor
        def _(pe):
            def arg_chunk(n, c, hs, s):
                fa, p = divmod(c, 2)
                bank = ARG_BANK[c]
                if not (isinstance(n, int) and n == 0 and c < 3):
                    pe.wait_ge(exp_done, n * CHUNKS + c - ARG_BACK[c] + 1)
                for j in range(2):
                    u = GU * hs + 2 * p + j
                    mm = nc.tensor.matmul(psA[:, bank, j * G:(j + 1) * G], a_diag[:, s, u * FA + fa].rearrange("p k b -> p (k b)"),
                                          q_st[:, s, u, :], start=True, stop=True)
                mm.then_inc(arg_done, 1)

            def group_ready(n, t, hs):
                if hs == 0:
                    pe.wait_ge(q_loaded, 16 * 8 * (t + 1))
                    pe.wait_ge(a_built, t + 1)

            def sums(i, e):
                pe.wait_ge(exp_done, (i + 1) * CHUNKS)
                pe.wait_ge(recip_done, i)
                for fa in range(FA):
                    for u in range(GU):
                        mm = nc.tensor.matmul(psS[32 * u:32 * u + 32, 0:G], ones_f[:], E[:, e, fa, u * G:(u + 1) * G],
                                              start=fa == 0, stop=fa == FA - 1)
                mm.then_inc(sum_done, 1)

            def spread(i, p):
                pe.wait_ge(recip_done, i + 1)
                pe.wait_ge(norm_done, 2 * i + p)
                for j in range(2):
                    mm = nc.tensor.matmul(psB[:, j * G:(j + 1) * G], bck[:, 2 * p + j, :], rS[:], start=True, stop=True)
                mm.then_inc(spread_done, 1)

            def ksum(i, b, h, s, e):
                pe.wait_ge(norm_done, 2 * i + b + 1)
                if b == 0:
                    pe.wait_ge(z_copied, i)
                for kh in range(2):
                    u = 2 * b + kh
                    for fa in range(FA):
                        q = min(fa, 3)
                        mm = nc.tensor.matmul(psZ[32 * q:32 * q + 32, b * G:(b + 1) * G], v_st[:, s, GU * h + u, fa, :],
                                              E[:, e, fa, u * G:(u + 1) * G],
                                              start=kh == 0 and fa < 4, stop=kh == 1 and fa != 3)
                if b == 1:
                    mm.then_inc(z_done, 1)

            def misc_free(T, j):
                if not (isinstance(T, int) and 6 * T + j < 2):
                    pe.wait_ge(misc_used, 6 * T + j - 1)

            def l0_transpose(T, j):
                if j == 0:
                    pe.wait_ge(y0_done, T + 1)
                misc_free(T, j)
                for c in range(4 * j, min(4 * j + 4, NCH0)):
                    n = min(CH0, C0 - c * CH0)
                    mm = nc.tensor.transpose(psM[0:n, j % 2, (c % 4) * P:(c % 4 + 1) * P], w0[:, c * CH0:c * CH0 + n], ident[:])
                mm.then_inc(misc_done, 1)

            def l0_product(T, c0, c1):
                if c0 == 0:
                    misc_free(T, 4)
                pe.wait_ge(misc_used, 6 * T + min((c1 - 1) // 4, 3) + 1)
                for c in range(c0, c1):
                    n = min(CH0, C0 - c * CH0)
                    mm = nc.tensor.matmul(psM[:, 0, 0:J], y0T[0:n, c, :], cw0_sb[0:n, c, :], start=c == 0, stop=c == NCH0 - 1)
                if c1 == NCH0:
                    mm.then_inc(misc_done, 1)

            def l0_ksum(T):
                misc_free(T, 5)
                pe.wait_ge(misc_used, 6 * T + 5)
                nc.tensor.matmul(psM[0:32, 1, 0:J], ones_k[:], o0[:], start=True, stop=True).then_inc(misc_done, 1)

            def body(t, s, eA, eB, sbk, nx2, nxt):
                T = t + SB_LEAD
                for h in range(2):
                    i = 2 * t + h
                    prev = not (isinstance(i, int) and i == 0)
                    before = (1, 1 - s, 2 * (1 - s) + 1) if h == 0 else (0, s, 2 * s)
                    args = nxt or h == 0
                    nh, ns = 1 - h, s if h == 0 else 1 - s

                    def chunks(*cs):
                        if args:
                            for c in cs:
                                arg_chunk(i + 1, c, nh, ns)

                    if prev:
                        spread(i - 1, 0)
                    if args:
                        group_ready(i + 1, t + 1, nh)
                    chunks(0, 1)
                    sums(i, 2 * s + h)
                    chunks(2, 3)
                    if sbk and h == 0:
                        l0_transpose(T, 0)
                        l0_transpose(T, 1)
                    if prev:
                        spread(i - 1, 1)
                    if sbk and h == 1:
                        l0_product(T, 6, 9)
                    chunks(4, 5)
                    if sbk and h == 0:
                        l0_transpose(T, 2)
                        l0_transpose(T, 3)
                    if prev:
                        ksum(i - 1, 0, *before)
                    if sbk and h == 1:
                        l0_product(T, 9, NCH0)
                    chunks(6, 7)
                    if sbk and h == 0:
                        l0_product(T, 0, 3)
                    if sbk and h == 1:
                        l0_ksum(T)
                    if prev:
                        ksum(i - 1, 1, *before)
                    chunks(8, 9)
                    if sbk and h == 0:
                        l0_product(T, 3, 6)

            pe.wait_ge(loaded, 16 * N_CONST)
            for T in range(SB_LEAD):
                for j in range(4):
                    l0_transpose(T, j)
                l0_product(T, 0, NCH0)
                l0_ksum(T)
            group_ready(0, 0, 0)
            pe.wait_ge(diag_zeroed, 1)
            pe.wait_ge(v_built, 1)
            for c in range(CHUNKS):
                arg_chunk(0, c, 0, 0)

            def body_v(t, s, eA, eB, sbk, nx2, nxt):
                if nxt:
                    pe.wait_ge(v_built, t + 1)
                else:
                    pe.wait_ge(v_built, TILES)
                body(t, s, eA, eB, sbk, nx2, nxt)

            tiles_of(pe, body_v)

            last = 2 * TILES - 1
            spread(last, 0)
            spread(last, 1)
            ksum(last, 0, 1, (TILES - 1) % 2, last % 4)
            ksum(last, 1, 1, (TILES - 1) % 2, last % 4)

            zb = E[:].rearrange("p (n s) a g -> p n (s a g)", n=2)
            pe.wait_ge(loaded_cw1, 16)
            for n in range(B // P):
                pe.wait_ge(z_loaded[n % 2], 16 * (n // 2 + 1))

                def product(r):
                    pe.wait_ge(f_cp, n * NCH1 // 4 + r + 1)
                    for c in range(4 * r, 4 * r + 4):
                        mm = nc.tensor.matmul(psZ[:, 0:J], y0T[0:CH1, (c % 8), :], big[0:CH1, c, :], start=c == 0, stop=c == NCH1 - 1)
                    mm.then_inc(f_mm, 1)

                for r in range(NCH1 // 4):
                    m = n * NCH1 // 4 + r
                    if m >= 2:
                        pe.wait_ge(f_cp, m - 1)
                    for c in range(4 * r, 4 * r + 4):
                        mm = nc.tensor.transpose(psM[0:CH1, r % 2, (c % 4) * P:(c % 4 + 1) * P], zb[:, n % 2, c * CH1:(c + 1) * CH1], ident[:])
                    mm.then_inc(f_tr, 1)
                    if r == 0 and n:
                        pe.wait_ge(f_out, n)
                    if r:
                        product(r - 1)
                product(NCH1 // 4 - 1)

        @block.scalar
        def _(act):
            def exps(n, e, cs):
                for c in cs:
                    act.wait_ge(arg_done, n * CHUNKS + c + 1)
                    if c == 0 and not (isinstance(n, int) and n < 4):
                        act.wait_ge(z_done, n - 3)
                    nc.scalar.activation(E[:, e, c // 2, (c % 2) * 2 * G:(c % 2 + 1) * 2 * G], psA[:, ARG_BANK[c], 0:2 * G],
                                         ACT.Exp).then_inc(exp_done, 1)

            def exp0(T, s):
                act.wait_ge(arg0_done, T + 1)
                nc.scalar.activation(arg0[:, s], arg0[:, s], ACT.Exp).then_inc(exp0_done, 1)

            def chunk_copy(T, j):
                act.wait_ge(misc_done, 6 * T + j + 1)
                if j == 3:
                    nc.scalar.copy(y0T[0:C0 - CH0 * 12, 12, :], psM[0:C0 - CH0 * 12, 1, 0:P]).then_inc(misc_used, 1)
                else:
                    nc.scalar.copy(y0T[0:CH0, 4 * j:4 * j + 4, :].rearrange("p c n -> p (c n)"), psM[0:CH0, j % 2, :]).then_inc(misc_used, 1)

            def out_copy(T):
                act.wait_ge(misc_done, 6 * T + 5)
                if not (isinstance(T, int) and T == 0):
                    act.wait_ge(q_read, T)
                nc.scalar.copy(o0[:], psM[:, 0, 0:J]).then_inc(misc_used, 1)

            def ks_copy(T, s):
                act.wait_ge(misc_done, 6 * T + 6)
                act.wait_ge(ks_stored, 16 * T)
                nc.scalar.copy(ks[:], psM[0:BT, 1, 0:J]).then_inc(misc_used, 1)

            def z_copy(i, h, n):
                act.wait_ge(z_done, i + 1)
                act.wait_ge(z_stored[h], 16 * FA * n)
                nc.scalar.copy(zS[:, h], psZ[:, 0:2 * G]).then_inc(z_copied, 1)

            def body(t, s, eA, eB, sbk, nx2, nxt):
                T = t + SB_LEAD
                for h in range(2):
                    i = 2 * t + h
                    args = nxt or h == 0
                    e = (2 * s + h + 1) % 4

                    def chunks(*cs):
                        if args:
                            exps(i + 1, e, cs)

                    chunks(0, 1, 2, 3)
                    if sbk and h == 0:
                        chunk_copy(T, 0)
                        chunk_copy(T, 1)
                    chunks(4, 5)
                    if sbk and h == 0:
                        chunk_copy(T, 2)
                        chunk_copy(T, 3)
                    if sbk and h == 1:
                        out_copy(T)
                    chunks(6, 7)
                    if sbk and h == 1:
                        ks_copy(T, s)
                    chunks(8, 9)
                    if not (isinstance(i, int) and i == 0):
                        z_copy(i - 1, h, t if h else t - 1)
                    if eA and h == 1:
                        exp0(t + A_LEAD, s)

            for T in range(A_LEAD):
                exp0(T, T % 2)
                if 1 <= T <= SB_LEAD:
                    for j in range(4):
                        chunk_copy(T - 1, j)
                    out_copy(T - 1)
                    ks_copy(T - 1, T - 1)
            exps(0, 0, range(CHUNKS))
            tiles_of(act, body)
            z_copy(2 * TILES - 1, 0, TILES - 1)
            for m in range(B // P * NCH1 // 4):
                act.wait_ge(f_tr, m + 1)
                if m >= 2:
                    act.wait_ge(f_mm, m - 1)
                nc.scalar.copy(y0T[0:CH1, 4 * (m % 2):4 * (m % 2) + 4, :].rearrange("p c n -> p (c n)"),
                               psM[0:CH1, m % 2, :]).then_inc(f_cp, 1)

        @block.gpsimd
        def _(pool):
            def build_a(t, s):
                pool.wait_ge(a_loaded, 16 * (NA + 1) * (t + 1))
                if not (isinstance(t, int) and t < 2):
                    pool.wait_ge(arg_done, 2 * CHUNKS * (t - 1))
                nc.gpsimd.tensor_tensor(a_diag[0:NA * KH, s],
                                        a_rep[:, s].unsqueeze(2).to_broadcast((NA * KH, U * FA, KH, FB)),
                                        dga[0:NA * KH].unsqueeze(1).unsqueeze(3).to_broadcast((NA * KH, U * FA, KH, FB)),
                                        ALU.mult).then_inc(a_built, 1)

            def build_v(t, s):
                pool.wait_ge(a_loaded, 16 * (NA + 1) * (t + 1))
                if not (isinstance(t, int) and t < 2):
                    pool.wait_ge(z_done, 2 * (t - 1))
                xt = xu[:, s].rearrange("p (b h a) -> p h b a", h=2, a=FA)
                vt = v_st[:, s].rearrange("p (b h) a c -> p h b a c", h=2)
                for kh in range(2):
                    for lo, hi, col in ((0, 4, 0), (4, 5, FB)):
                        last = nc.gpsimd.tensor_tensor(vt[:, kh, :, lo:hi, col:col + FB],
                                                       xt[:, kh, :, lo:hi].unsqueeze(3).to_broadcast((P, U // 2, hi - lo, FB)),
                                                       wv_mask[:, kh, lo:hi].unsqueeze(1).to_broadcast((P, U // 2, hi - lo, FB)), ALU.mult)
                last.then_inc(v_built, 1)

            def product0(T, s):
                pool.wait_ge(ew_step, EW_STEPS * T + 3)
                if not (isinstance(T, int) and T < 2):
                    pool.wait_ge(y0_done, T - 1)
                nc.gpsimd.tensor_tensor(arg0[:, s].rearrange("p (f g) -> p f g", f=F), s0[:, s, 0].unsqueeze(2).to_broadcast((P, F, F)),
                                        s0[:, s, 1].unsqueeze(1).to_broadcast((P, F, F)), ALU.mult).then_inc(prod0, 1)

            def weights0(T, s):
                pool.wait_ge(recip0_done, T + 1)
                if not (isinstance(T, int) and T == 0):
                    pool.wait_ge(misc_done, 6 * T - 2)
                nc.gpsimd.tensor_tensor(w0[:].rearrange("p (f g) -> p f g", f=F), s0[:, s, 2].unsqueeze(2).to_broadcast((P, F, F)),
                                        s0[:, s, 5].unsqueeze(1).to_broadcast((P, F, F)), ALU.mult).then_inc(w0_done, 1)

            def apply0(T, s):
                pool.wait_ge(w0_done, T + 1)
                nc.gpsimd.tensor_tensor(w0[:], arg0[:, s], w0[:], ALU.mult).then_inc(y0_done, 1)

            for T in range(A_LEAD):
                product0(T, T % 2)
                if T < EW_LEAD:
                    weights0(T, T % 2)
                    apply0(T, T % 2)
            pool.wait_ge(loaded, 16 * N_CONST)
            nc.gpsimd.memset(v_st[:], 0.0).then_inc(mask_ready, 1)
            for kh in range(2):
                nc.gpsimd.tensor_tensor(wv_mask[:, kh], wvu[:, kh].unsqueeze(2).to_broadcast((P, FA, FB)),
                                        fbm[:].unsqueeze(1).to_broadcast((P, FA, FB)), ALU.mult).then_inc(mask_ready, 1)
            for s in range(2):
                pool.wait_ge(mask_ready, 3 + s)
                nc.gpsimd.tensor_copy(a_diag[NA * KH:P, s], dga[NA * KH:P].unsqueeze(1).unsqueeze(3).to_broadcast(
                    (2 * KH, U * FA, KH, FB))).then_inc(mask_ready, 1)
            pool.wait_ge(mask_ready, 5)
            nc.gpsimd.sem_inc(diag_zeroed, 1)
            build_v(0, 0)
            build_a(0, 0)
            build_a(1, 1)

            def body(t, s, eA, eB, sbk, nx2, nxt):
                if eB:
                    weights0(t + EW_LEAD, 1 - s)
                    apply0(t + EW_LEAD, 1 - s)
                if eA:
                    product0(t + A_LEAD, s)
                if nxt:
                    build_v(t + 1, 1 - s)
                if nx2:
                    build_a(t + 2, s)

            tiles_of(pool, body)

        @block.vector
        def _(dve):
            def w(n, width):
                return w_sb[:, n, 0:width]

            v = nc.vector
            x3 = xr.rearrange("p (t f) -> p t f", f=F)
            a3 = a1.rearrange("p (t f) -> p t f", f=F)

            def prepare(step):
                if step == 0:
                    dve.wait_ge(loaded_x, 16)
                    v.tensor_tensor(a3, x3, w(3, F).unsqueeze(1).to_broadcast((P, TILES, F)), ALU.mult).then_inc(prep, 1)
                    dve.wait_ge(prep, 1)
                    v.tensor_copy(a_hi, a1).then_inc(a_split, 1)
                    v.tensor_reduce(amx[:], a3, AX.X, ALU.max).then_inc(prep, 1)
                elif step == 1:
                    v.tensor_reduce(amn[:], a3, AX.X, ALU.min).then_inc(prep, 1)
                    dve.wait_ge(a_split, 1)
                    dve.wait_ge(prep, 3)
                    v.tensor_tensor(a1, a1, a_hi, ALU.subtract).then_inc(prep, 1)
                elif step == 2:
                    dve.wait_ge(prep, 4)
                    v.tensor_copy(a_md, a1).then_inc(a_split, 1)
                    dve.wait_ge(a_split, 2)
                    v.tensor_tensor(a1, a1, a_md, ALU.subtract).then_inc(prep, 1)
                    dve.wait_ge(prep, 5)
                    v.tensor_copy(a_lo, a1).then_inc(a_split, 1)

            def ew_small(T, s):
                a0, q0, v0, m0, t0 = (s0[:, s, n] for n in range(5))
                dve.wait_ge(loaded_x0, 16 * (T + 1))
                v.tensor_tensor(a0, xt0[:], w(1, F), ALU.mult).then_inc(ew_step, 1)
                v.tensor_tensor(q0, xt0[:], w(0, F), ALU.mult).then_inc(ew_step, 1)
                v.tensor_tensor(v0, xt0[:], w(2, F), ALU.mult).then_inc(ew_step, 1)
                dve.wait_ge(ew_step, EW_STEPS * T + 3)
                v.tensor_reduce(s0m[:, 0:1], a0, AX.X, ALU.max).then_inc(ew_step, 1)
                v.tensor_reduce(s0m[:, 1:2], a0, AX.X, ALU.min).then_inc(ew_step, 1)
                dve.wait_ge(ew_step, EW_STEPS * T + 5)
                v.tensor_scalar(t0, q0, s0m[:, 0:1], None, ALU.mult).then_inc(ew_step, 1)
                dve.wait_ge(ew_step, EW_STEPS * T + 6)
                v.scalar_tensor_tensor(out=m0, in0=q0, scalar=s0m[:, 1:2], in1=t0, op0=ALU.mult, op1=ALU.max).then_inc(ew_step, 1)

            def ew_shift(T, s):
                dve.wait_ge(ew_step, EW_STEPS * T + 7)
                dve.wait_ge(prod0, T + 1)
                p3 = arg0[:, s].rearrange("p (f g) -> p f g", f=F)
                v.tensor_tensor(p3, p3, s0[:, s, 3].unsqueeze(1).to_broadcast((P, F, F)), ALU.subtract).then_inc(arg0_done, 1)

            def ew_sum(T, s):
                dve.wait_ge(exp0_done, T + 1)
                v.tensor_reduce(s0[:, s, 4], arg0[:, s].rearrange("p (f g) -> p g f", f=F), AX.X, ALU.add).then_inc(sum0_done, 1)
                dve.wait_ge(sum0_done, T + 1)
                v.reciprocal(s0[:, s, 5], s0[:, s, 4]).then_inc(recip0_done, 1)

            def q_parts_of(T, s):
                dve.wait_ge(misc_used, 6 * T + 6)
                if not (isinstance(T, int) and T < 2):
                    dve.wait_ge(q_stored, 16 * (T - 1))
                q, m, r = (qf[:, n, :] for n in range(3))
                at = Q_STEPS * T
                v.tensor_tensor(q, o0[:], w(4, G), ALU.mult).then_inc(q_chain, 1)
                dve.wait_ge(q_chain, at + 1)
                v.tensor_scalar(m, q, amx[:, bass.ds(T, 1)], None, ALU.mult).then_inc(q_chain, 1)
                v.tensor_copy(q_out[:, s, 0, :], q).then_inc(q_chain, 1)
                dve.wait_ge(q_chain, at + 3)
                v.scalar_tensor_tensor(out=m, in0=q, scalar=amn[:, bass.ds(T, 1)], in1=m, op0=ALU.mult, op1=ALU.max).then_inc(q_chain, 1)
                v.tensor_tensor(r, q, q_out[:, s, 0, :], ALU.subtract).then_inc(q_chain, 1)
                dve.wait_ge(q_chain, at + 5)
                v.tensor_copy(q_out[:, s, 3, :], m).then_inc(q_chain, 1)
                v.tensor_copy(q_out[:, s, 1, :], r).then_inc(q_chain, 1)
                dve.wait_ge(q_chain, at + 7)
                v.tensor_tensor(m, m, q_out[:, s, 3, :], ALU.subtract).then_inc(q_chain, 1)
                v.tensor_tensor(r, r, q_out[:, s, 1, :], ALU.subtract).then_inc(q_chain, 1)
                dve.wait_ge(q_chain, at + 9)
                v.tensor_copy(q_out[:, s, 4, :], m).then_inc(q_chain, 1)
                v.tensor_copy(q_out[:, s, 2, :], r).then_inc(q_chain, 1)
                dve.wait_ge(q_chain, at + 11)
                dve.sem_inc(q_split, 1)
                dve.sem_inc(q_read, 1)

            def recip(i):
                dve.wait_ge(sum_done, i + 1)
                dve.wait_ge(spread_done, 2 * i)
                v.reciprocal(rS[:], psS[:, 0:G]).then_inc(recip_done, 1)

            def normalise(i, p, e):
                dve.wait_ge(spread_done, 2 * i + p + 1)
                x = E[:, e, :, p * 2 * G:(p + 1) * 2 * G]
                v.tensor_tensor(x, x, psB[:, 0:2 * G].unsqueeze(1).to_broadcast((P, FA, 2 * G)), ALU.mult).then_inc(norm_done, 1)

            def body(t, s, eA, eB, sbk, nx2, nxt):
                A, X, Q = t + A_LEAD, t + EW_LEAD, t + SB_LEAD
                i = 2 * t
                prev = not (isinstance(t, int) and t == 0)
                if prev:
                    normalise(i - 1, 0, 2 * (1 - s) + 1)
                if eB:
                    ew_sum(X, 1 - s)
                if prev:
                    normalise(i - 1, 1, 2 * (1 - s) + 1)
                recip(i)
                if eA:
                    ew_small(A, s)
                normalise(i, 0, 2 * s)
                normalise(i, 1, 2 * s)
                recip(i + 1)
                if eA:
                    ew_shift(A, s)
                if sbk:
                    q_parts_of(Q, s)

            for T in range(A_LEAD):
                if T == 0:
                    dve.wait_ge(loaded_w, 16)
                ew_small(T, T % 2)
                if T == 0:
                    prepare(0)
                ew_shift(T, T % 2)
                if T == 0:
                    prepare(1)
                if T < EW_LEAD:
                    ew_sum(T, T % 2)
                if T == 0:
                    prepare(2)
                if 1 <= T <= SB_LEAD:
                    q_parts_of(T - 1, T - 1)
            tiles_of(dve, body)
            for p in range(2):
                normalise(2 * TILES - 1, p, (2 * TILES - 1) % 4)
            for n in range(B // P):
                dve.wait_ge(f_mm, (n + 1) * NCH1 // 4)
                v.tensor_copy(w0[:, n * J:(n + 1) * J], psZ[:, 0:J]).then_inc(f_out, 1)


def kernel(r_inputs, L0_rec_wq0, L0_rec_wk0, L0_rec_wv0, L0_rec_cw0, L0_rec_wq1, L0_rec_wk1, L0_rec_wv1, L0_rec_cw1):
    import numpy as np
    import ml_dtypes
    import concourse.bacc as bacc
    from concourse.bass_utils import run_bass_kernel_spmd

    x = np.asarray(r_inputs)
    c = np.ascontiguousarray
    rows = x.transpose(0, 2, 1).reshape(TILES, P, F)
    x_rows = c(rows.transpose(1, 0, 2).reshape(P, TILES * F))
    x_units = c(x.reshape(TILES, BT, FA, FB, 2, KH).transpose(5, 3, 0, 1, 4, 2).reshape(P, TILES * U * FA))
    w_rows = np.zeros((P, 5, G), np.float32)
    for n, wt in enumerate((L0_rec_wq0, L0_rec_wk0, L0_rec_wv0, L0_rec_wk1, L0_rec_wq1)):
        wt = np.asarray(wt)[0].T
        w_rows[:, n, :wt.shape[1]] = np.tile(wt, (BT, 1))
    wv_units = c(np.asarray(L0_rec_wv1)[0].reshape(FA, FB, 2, KH).transpose(3, 1, 2, 0).reshape(P, 2, FA))
    p = np.arange(P)
    ident = np.eye(P, dtype=np.float32)
    diag_a = (p[:, None] % KH == np.arange(KH)).astype(np.float32)
    diag_a[NA * KH:] *= -1
    sum_f = (p[:, None] // FB == np.arange(32) % KH).astype(np.float32)
    bcast_k = np.zeros((P, GU, P), np.float32)
    for u in range(GU):
        bcast_k[32 * u + p // FB, u, p] = 1
    sum_k = (p[:, None] // K == np.arange(32)).astype(np.float32)
    fb_mask = (p[:, None] % FB == np.arange(FB)).astype(np.float32)
    arrays = {
        "x_rows": x_rows, "x_units": x_units, "w_rows": w_rows, "wv_units": wv_units,
        "cw0": c(np.asarray(L0_rec_cw0)[0]), "cw1": c(np.asarray(L0_rec_cw1)[0]),
        "ident_d": ident, "diag_a": diag_a.astype(ml_dtypes.bfloat16), "sum_f": sum_f, "bcast_k": bcast_k,
        "sum_k": sum_k, "fb_mask": fb_mask,
    }
    nc = bacc.Bacc("TRN2", target_bir_lowering=False, num_devices=1)
    args = {n: nc.dram_tensor(n, a.shape, mybir.dt.from_np(a.dtype), kind="ExternalInput").ap() for n, a in arrays.items()}
    out = nc.dram_tensor("out", (B, 2 * J), mybir.dt.float32, kind="ExternalOutput").ap()
    cin_kernel(nc, *args_in_order(args), out)
    r = run_bass_kernel_spmd(nc, [arrays], core_ids=[0])
    return r.results[0]["out"]


def args_in_order(args):
    return [args[n] for n in ("x_rows", "x_units", "w_rows", "wv_units", "cw0", "cw1", "ident_d", "diag_a", "sum_f",
                              "bcast_k", "sum_k", "fb_mask")]
```

```python
import concourse.bass as bass
from concourse import mybir
from contextlib import ExitStack

B, F, K, J = 512, 40, 32, 200
G = J
P = 128
TILES = B * K // P
BT = P // K
KH = 16
U = P // KH
FA, FB = 5, 8
GU = 4
A_TERMS = (0, 0, -1, 1, 1, 2, -1, 0)
Q_TERMS = (0, 1, 2, 0, 1, 0, 3, 4)
TERMS = 8
C0 = F * F
CH0 = 124
NCH0 = -(-C0 // CH0)
C1, CH1 = F * G, 125
NCH1 = C1 // CH1
CHUNKS = FA * 2
ARG_BANK = [0, 1, 2, 0, 1, 2, 0, 1, 2, 1]
ARG_BACK = [4, 2, 4, 3, 3, 3, 3, 3, 3, 2]
A_LEAD, EW_LEAD, SB_LEAD = 4, 3, 2
EW_STEPS = 7
Q_STEPS, Q_CASTS = 5, 6


def cin_kernel(nc, x_rows, x_units, w_rows, wv_units, cw0, cw1, ident_d, diag_a, sum_f, bcast_k, sum_k, lo_rows_d, fb_mask, out):
    f32, bf16, f32r = mybir.dt.float32, mybir.dt.bfloat16, mybir.dt.float32r
    ALU, ACT, AX = mybir.AluOpType, mybir.ActivationFunctionType, mybir.AxisListType

    with ExitStack() as ctx:
        def sb(name, shape, dt=f32):
            return ctx.enter_context(nc.sbuf_tensor(name, shape, dt))

        def pb(name, shape):
            return ctx.enter_context(nc.psum_tensor(name, shape, f32))

        def sem(name):
            return ctx.enter_context(nc.semaphore(name))

        a_parts = nc.dram_tensor("a_parts", (P, TERMS, TILES * F), bf16, kind="Internal").ap()
        q_parts = nc.dram_tensor("q_parts", (2, P, TERMS, G), bf16, kind="Internal").ap()
        z_dram = nc.dram_tensor("z_dram", (B, F, G), f32, kind="Internal").ap()

        xt0 = sb("xt0", [P, F])
        xu = sb("xu", [P, 2, U * FA])
        w_sb = sb("w_sb", [P, 4 * F + G])
        wvu = sb("wvu", [P, 2, FA])
        wv_mask = sb("wv_mask", [P, 2, FA, FB])
        fbm = sb("fbm", [P, FB])
        cw0_sb = sb("cw0_sb", [P, NCH0, J])
        big = sb("big", [P, NCH1, J])
        ident = sb("ident", [P, P])
        dga = sb("dga", [P, KH], bf16)
        ones_f = sb("ones_f", [P, 32])
        bck = sb("bck", [P, GU, P], f32r)
        ones_k = sb("ones_k", [P, 32])
        amx = sb("amx", [P, TILES])
        amn = sb("amn", [P, TILES])
        E = sb("E", [P, 4, FA, GU * G])
        a_rep = sb("a_rep", [P, 2, U * FA, FB], bf16)
        a_diag = sb("a_diag", [P, 2, U * FA, KH, FB], bf16)
        q_st = sb("q_st", [P, 2, U, G], bf16)
        q_out = sb("q_out", [P, 2, 5, G], bf16)
        v_st = sb("v_st", [P, 2, U, FA, 32])
        lo_rows = sb("lo_rows", [P, 1])
        rS = sb("rS", [P, G])
        r_hi = sb("r_hi", [P, G], f32r)
        r_halves = sb("r_halves", [P, G], f32r)
        zS = sb("zS", [P, 2, 2 * G])
        ks = sb("ks", [BT, J])
        s0 = sb("s0", [P, 2, 6, F])
        s0m = sb("s0m", [P, 2])
        arg0 = sb("arg0", [P, 2, C0])
        w0 = sb("w0", [P, C0])
        y0T = sb("y0T", [P, NCH0, P])
        o0 = sb("o0", [P, J])
        qf = sb("qf", [P, 3, G])

        bigf = big[:].rearrange("p c j -> p (c j)")
        NX = TILES * F
        a1 = bigf[:, 0:NX]
        xr = E[:].rearrange("p s a g -> p (s a g)")[:, 0:NX]
        a_hi = bigf[:, NX:NX + NX // 2].bitcast(bf16)
        a_md = bigf[:, NX + NX // 2:2 * NX].bitcast(bf16)
        minus = E[:].rearrange("p s a g -> p (s a g)")[:, NX:NX + NX // 2].bitcast(bf16)
        bck_f = E[:].rearrange("p s a g -> p (s a g)")[:, NX + NX // 2:NX + NX // 2 + GU * P]
        a_lo = bigf[:, 2 * NX:2 * NX + NX // 2].bitcast(bf16)

        psA = pb("psA", [P, 3, 512])
        psS = pb("psS", [P, 512])
        psB = pb("psB", [P, 512])
        psZ = pb("psZ", [P, 512])
        psM = pb("psM", [P, 2, 512])

        loaded = sem("loaded")
        loaded_x = sem("loaded_x")
        loaded_x0 = sem("loaded_x0")
        loaded_w = sem("loaded_w")
        loaded_cw1 = sem("loaded_cw1")
        prep = sem("prep")
        a_split = sem("a_split")
        a_stored = sem("a_stored")
        mask_ready = sem("mask_ready")
        a_loaded = sem("a_loaded")
        a_built = sem("a_built")
        v_built = sem("v_built")
        q_stored = sem("q_stored")
        q_loaded = sem("q_loaded")
        arg_done = sem("arg_done")
        exp_done = sem("exp_done")
        sum_done = sem("sum_done")
        recip_done = sem("recip_done")
        hi_done = sem("hi_done")
        halves_done = sem("halves_done")
        bck_ready = sem("bck_ready")
        spread_done = sem("spread_done")
        norm_done = sem("norm_done")
        z_done = sem("z_done")
        z_copied = sem("z_copied")
        z_stored = [sem(f"z_stored{h}") for h in range(2)]
        ew_step = sem("ew_step")
        prod0 = sem("prod0")
        sum0_done = sem("sum0_done")
        arg0_done = sem("arg0_done")
        exp0_done = sem("exp0_done")
        recip0_done = sem("recip0_done")
        w0_done = sem("w0_done")
        y0_done = sem("y0_done")
        misc_done = sem("misc_done")
        misc_used = sem("misc_used")
        q_steps = sem("q_steps")
        q_casts = sem("q_casts")
        ks_stored = sem("ks_stored")
        z_loaded = [sem(f"z_loaded{n}") for n in range(2)]
        f_tr = sem("f_tr")
        f_cp = sem("f_cp")
        f_mm = sem("f_mm")
        f_out = sem("f_out")
        out_stored = sem("out_stored")

        block = ctx.enter_context(nc.Block())
        NLOOP = (TILES - 6) // 2

        def tiles_of(engine, body):
            for t in range(2):
                body(t, t, True, True, True, True, True)
            with engine.Fori(1, NLOOP) as pair:
                for s in range(2):
                    body(pair * 2 + s, s, True, True, True, True, True)
            for t in range(2 * NLOOP, TILES):
                body(t, t % 2, t + A_LEAD < TILES, t + EW_LEAD < TILES, t + SB_LEAD < TILES, t + 2 < TILES, t + 1 < TILES)

        N_CONST = 10

        @block.sync
        def _(sp):
            sp.dma_start(xt0[:], x_rows[:, 0:F]).then_inc(loaded_x0, 16)
            sp.dma_start(w_sb[:], w_rows).then_inc(loaded_w, 16)
            sp.dma_start(xr, x_rows).then_inc(loaded_x, 16)
            for dst, src in ((ident[:], ident_d), (dga[:], diag_a), (ones_f[:], sum_f), (bck_f, bcast_k), (ones_k[:], sum_k),
                             (lo_rows[:], lo_rows_d), (fbm[:], fb_mask), (wvu[:], wv_units)):
                sp.dma_start(dst, src).then_inc(loaded, 16)
            sp.dma_start(cw0_sb[0:CH0, 0:NCH0 - 1, :], cw0[0:CH0 * (NCH0 - 1)].rearrange("(c p) j -> p c j", p=CH0)).then_inc(loaded, 16)
            sp.dma_start(cw0_sb[0:C0 - CH0 * (NCH0 - 1), NCH0 - 1, :], cw0[CH0 * (NCH0 - 1):C0]).then_inc(loaded, 16)
            sp.wait_ge(ew_step, 3)
            sp.dma_start(xt0[:], x_rows[:, F:2 * F]).then_inc(loaded_x0, 16)
            sp.wait_ge(a_split, 4)
            for n, part in enumerate(A_TERMS):
                src = minus if part < 0 else (a_hi, a_md, a_lo)[part]
                sp.dma_start(a_parts[:, n], src).then_inc(a_stored, 16)
            sp.wait_ge(a_stored, 16 * TERMS)

            def load_a(t, s):
                sp.dma_start(xu[:, s], x_units[:, bass.ds(t * U * FA, U * FA)]).then_inc(a_loaded, 16)
                sp.dma_start(a_rep[:, s].rearrange("p (u a) b -> p u (a b)", u=U),
                             a_parts[:, :, bass.ds(t * F, F)].rearrange("(u k) n f -> (k n) u f", k=KH)).then_inc(a_loaded, 16)

            def move_q(t, s):
                for a, b, n, casts in ((0, 3, 0, Q_CASTS - 2), (0, 2, 3, None), (0, 1, 5, None), (3, 5, 6, Q_CASTS)):
                    if casts is not None:
                        sp.wait_ge(q_casts, Q_CASTS * t + casts)
                    sp.dma_start(q_parts[s, :, n:n + b - a], q_out[:, s, a:b]).then_inc(q_stored, 16)
                sp.wait_ge(q_stored, 64 * (t + 1))
                sp.dma_start(q_st[:, s], q_parts[s].rearrange("(u k) n g -> (k n) u g", k=KH)).then_inc(q_loaded, 16)

            def load_x0(T):
                sp.dma_start(xt0[:], x_rows[:, bass.ds(T * F, F)]).then_inc(loaded_x0, 16)

            load_a(0, 0)
            for T in range(2, A_LEAD + 1):
                if T == A_LEAD:
                    for n in range(SB_LEAD):
                        sp.wait_ge(misc_used, 6 * (n + 1))
                        sp.dma_start(out[n * BT:(n + 1) * BT, 0:J], ks[:]).then_inc(ks_stored, 16)
                        if n == 0:
                            move_q(0, 0)
                            sp.wait_ge(ks_stored, 16)
                sp.wait_ge(ew_step, EW_STEPS * (T - 1) + 3)
                load_x0(T)
            sp.wait_ge(a_loaded, 32)
            load_a(1, 1)
            sp.wait_ge(a_loaded, 64)
            sp.dma_start(big[0:CH1], cw1.rearrange("(c p) j -> p c j", p=CH1)).then_inc(loaded_cw1, 16)

            def body(t, s, eA, eB, sbk, nx2, nxt):
                if nx2:
                    sp.wait_ge(v_built, t + 1)
                    load_a(t + 2, s)
                if nxt:
                    move_q(t + 1, 1 - s)
                if eA and not (isinstance(t, int) and t + A_LEAD + 1 >= TILES):
                    sp.wait_ge(ew_step, EW_STEPS * (t + A_LEAD) + 3)
                    load_x0(t + A_LEAD + 1)
                if not (isinstance(t, int) and t == 0):
                    store_z(2 * t - 1, 0)
                store_z(2 * t, 1, t if nx2 else None)
                if sbk:
                    sp.wait_ge(misc_used, 6 * (t + SB_LEAD + 1))
                    sp.dma_start(out[bass.ds((t + SB_LEAD) * BT, BT), 0:J], ks[:]).then_inc(ks_stored, 16)

            def store_z(i, h, t=None):
                sp.wait_ge(z_copied, i + 1)
                zd = z_dram[bass.ds(2 * i, 2)]
                for fa in range(FA):
                    if fa == 1 and t is not None:
                        sp.wait_ge(a_loaded, 32 * (t + 3))
                    if fa == 2 and t is not None:
                        sp.wait_ge(ks_stored, 16 * (t + 2))
                    row = 32 * fa if fa < 4 else 96 + FB
                    sp.dma_start(zd[:, fa * FB:(fa + 1) * FB, :].rearrange("b f g -> f b g"),
                                 zS[row:row + FB, h].rearrange("f (b g) -> f b g", b=2)).then_inc(z_stored[h], 16)

            tiles_of(sp, body)
            sp.wait_ge(ks_stored, 16 * TILES)
            zb = E[:].rearrange("p (n s) a g -> p n (s a g)", n=2)
            for n in range(B // P):
                if n == 0:
                    sp.wait_ge(z_done, 2 * TILES - 2)
                    for h in range(2):
                        sp.wait_ge(z_stored[h], 16 * FA * (TILES - 2))
                if n == 1:
                    sp.wait_ge(z_done, 2 * TILES)
                if n == B // P - 1:
                    store_z(2 * TILES - 1, 0)
                    for h in range(2):
                        sp.wait_ge(z_stored[h], 16 * FA * TILES)
                if n > 1:
                    sp.wait_ge(f_tr, (n - 1) * NCH1 // 4)
                sp.dma_start(zb[:, n % 2], z_dram[n * P:(n + 1) * P].rearrange("b f g -> b (f g)")).then_inc(z_loaded[n % 2], 16)
            for n in range(B // P):
                sp.wait_ge(f_out, n + 1)
                sp.dma_start(out[n * P:(n + 1) * P, J:2 * J], w0[:, n * J:(n + 1) * J]).then_inc(out_stored, 16)
            sp.wait_ge(out_stored, 16 * (B // P))

        @block.tensor
        def _(pe):
            def arg_chunk(n, c, hs, s):
                fa, p = divmod(c, 2)
                bank = ARG_BANK[c]
                if not (isinstance(n, int) and n == 0 and c < 3):
                    pe.wait_ge(exp_done, n * CHUNKS + c - ARG_BACK[c] + 1)
                for j in range(2):
                    u = GU * hs + 2 * p + j
                    mm = nc.tensor.matmul(psA[:, bank, j * G:(j + 1) * G], a_diag[:, s, u * FA + fa].rearrange("p k b -> p (k b)"),
                                          q_st[:, s, u, :], start=True, stop=True)
                mm.then_inc(arg_done, 1)

            def group_ready(n, t, hs):
                if hs == 0:
                    pe.wait_ge(q_loaded, 16 * (t + 1))
                    pe.wait_ge(a_built, t + 1)

            def sums(i, e):
                pe.wait_ge(exp_done, (i + 1) * CHUNKS)
                pe.wait_ge(recip_done, i)
                for fa in range(FA):
                    for u in range(GU):
                        mm = nc.tensor.matmul(psS[32 * u:32 * u + 32, 0:G], ones_f[:], E[:, e, fa, u * G:(u + 1) * G],
                                              start=fa == 0, stop=fa == FA - 1)
                mm.then_inc(sum_done, 1)

            def spread(i, p):
                pe.wait_ge(halves_done, i + 1)
                pe.wait_ge(norm_done, 2 * i + p)
                for j in range(2):
                    mm = nc.tensor.matmul(psB[:, j * G:(j + 1) * G], bck[:, 2 * p + j, :], r_halves[:], start=True, stop=True)
                mm.then_inc(spread_done, 1)

            def ksum(i, b, h, s, e):
                pe.wait_ge(norm_done, 2 * i + b + 1)
                if b == 0:
                    pe.wait_ge(z_copied, i)
                for kh in range(2):
                    u = 2 * b + kh
                    for fa in range(FA):
                        q = min(fa, 3)
                        mm = nc.tensor.matmul(psZ[32 * q:32 * q + 32, b * G:(b + 1) * G], v_st[:, s, GU * h + u, fa, :],
                                              E[:, e, fa, u * G:(u + 1) * G],
                                              start=kh == 0 and fa < 4, stop=kh == 1 and fa != 3)
                if b == 1:
                    mm.then_inc(z_done, 1)

            def misc_free(T, j):
                if not (isinstance(T, int) and 6 * T + j < 2):
                    pe.wait_ge(misc_used, 6 * T + j - 1)

            def l0_transpose(T, j):
                if j == 0:
                    pe.wait_ge(y0_done, T + 1)
                misc_free(T, j)
                for c in range(4 * j, min(4 * j + 4, NCH0)):
                    n = min(CH0, C0 - c * CH0)
                    mm = nc.tensor.transpose(psM[0:n, j % 2, (c % 4) * P:(c % 4 + 1) * P], w0[:, c * CH0:c * CH0 + n], ident[:])
                mm.then_inc(misc_done, 1)

            def l0_product(T, c0, c1):
                if c0 == 0:
                    misc_free(T, 4)
                pe.wait_ge(misc_used, 6 * T + min((c1 - 1) // 4, 3) + 1)
                for c in range(c0, c1):
                    n = min(CH0, C0 - c * CH0)
                    mm = nc.tensor.matmul(psM[:, 0, 0:J], y0T[0:n, c, :], cw0_sb[0:n, c, :], start=c == 0, stop=c == NCH0 - 1)
                if c1 == NCH0:
                    mm.then_inc(misc_done, 1)

            def l0_ksum(T):
                misc_free(T, 5)
                pe.wait_ge(misc_used, 6 * T + 5)
                nc.tensor.matmul(psM[0:32, 1, 0:J], ones_k[:], o0[:], start=True, stop=True).then_inc(misc_done, 1)

            def body(t, s, eA, eB, sbk, nx2, nxt):
                T = t + SB_LEAD
                for h in range(2):
                    i = 2 * t + h
                    prev = not (isinstance(i, int) and i == 0)
                    before = (1, 1 - s, 2 * (1 - s) + 1) if h == 0 else (0, s, 2 * s)
                    args = nxt or h == 0
                    nh, ns = 1 - h, s if h == 0 else 1 - s

                    def chunks(*cs):
                        if args:
                            for c in cs:
                                arg_chunk(i + 1, c, nh, ns)

                    if prev:
                        spread(i - 1, 0)
                    if h == 0:
                        chunks(0, 1)
                    sums(i, 2 * s + h)
                    if sbk and h == 1:
                        l0_product(T, 8, 11)
                    if prev and h == 1:
                        spread(i - 1, 1)
                    if h == 1:
                        if args:
                            group_ready(i + 1, t + 1, nh)
                        chunks(0, 1)
                    if sbk and h == 1:
                        l0_product(T, 11, NCH0)
                    chunks(2, 3)
                    if sbk and h == 0:
                        l0_transpose(T, 0)
                        l0_transpose(T, 1)
                    if prev and h == 0:
                        spread(i - 1, 1)
                    chunks(4, 5)
                    if sbk and h == 0:
                        l0_transpose(T, 2)
                        l0_transpose(T, 3)
                    if prev:
                        ksum(i - 1, 0, *before)
                    chunks(6, 7)
                    if sbk and h == 0:
                        l0_product(T, 0, 4)
                    if sbk and h == 1:
                        l0_ksum(T)
                    if prev:
                        ksum(i - 1, 1, *before)
                    chunks(8, 9)
                    if sbk and h == 0:
                        l0_product(T, 4, 8)

            pe.wait_ge(loaded, 16 * N_CONST)
            pe.wait_ge(bck_ready, 1)
            for T in range(SB_LEAD):
                for j in range(4):
                    l0_transpose(T, j)
                l0_product(T, 0, NCH0)
                l0_ksum(T)
            group_ready(0, 0, 0)
            pe.wait_ge(v_built, 1)
            for c in range(CHUNKS):
                arg_chunk(0, c, 0, 0)

            def body_v(t, s, eA, eB, sbk, nx2, nxt):
                if nxt:
                    pe.wait_ge(v_built, t + 1)
                else:
                    pe.wait_ge(v_built, TILES)
                body(t, s, eA, eB, sbk, nx2, nxt)

            tiles_of(pe, body_v)

            last = 2 * TILES - 1
            spread(last, 0)
            spread(last, 1)
            ksum(last, 0, 1, (TILES - 1) % 2, last % 4)
            ksum(last, 1, 1, (TILES - 1) % 2, last % 4)

            zb = E[:].rearrange("p (n s) a g -> p n (s a g)", n=2)
            pe.wait_ge(loaded_cw1, 16)
            for n in range(B // P):
                pe.wait_ge(z_loaded[n % 2], 16 * (n // 2 + 1))

                def product(r):
                    pe.wait_ge(f_cp, n * NCH1 // 4 + r + 1)
                    for c in range(4 * r, 4 * r + 4):
                        mm = nc.tensor.matmul(psZ[:, 0:J], y0T[0:CH1, (c % 8), :], big[0:CH1, c, :], start=c == 0, stop=c == NCH1 - 1)
                    mm.then_inc(f_mm, 1)

                for r in range(NCH1 // 4):
                    m = n * NCH1 // 4 + r
                    if m >= 2:
                        pe.wait_ge(f_cp, m - 1)
                    for c in range(4 * r, 4 * r + 4):
                        mm = nc.tensor.transpose(psM[0:CH1, r % 2, (c % 4) * P:(c % 4 + 1) * P], zb[:, n % 2, c * CH1:(c + 1) * CH1], ident[:])
                    mm.then_inc(f_tr, 1)
                    if r == 0 and n:
                        pe.wait_ge(f_out, n)
                    if r:
                        product(r - 1)
                product(NCH1 // 4 - 1)

        @block.scalar
        def _(act):
            def exps(n, e, cs):
                for c in cs:
                    act.wait_ge(arg_done, n * CHUNKS + c + 1)
                    if c == 0 and not (isinstance(n, int) and n < 4):
                        act.wait_ge(z_done, n - 3)
                    nc.scalar.activation(E[:, e, c // 2, (c % 2) * 2 * G:(c % 2 + 1) * 2 * G], psA[:, ARG_BANK[c], 0:2 * G],
                                         ACT.Exp).then_inc(exp_done, 1)

            def exp0(T, s):
                act.wait_ge(arg0_done, T + 1)
                nc.scalar.activation(arg0[:, s], arg0[:, s], ACT.Exp).then_inc(exp0_done, 1)

            def chunk_copy(T, j):
                act.wait_ge(misc_done, 6 * T + j + 1)
                if j == 3:
                    nc.scalar.copy(y0T[0:C0 - CH0 * 12, 12, :], psM[0:C0 - CH0 * 12, 1, 0:P]).then_inc(misc_used, 1)
                else:
                    nc.scalar.copy(y0T[0:CH0, 4 * j:4 * j + 4, :].rearrange("p c n -> p (c n)"), psM[0:CH0, j % 2, :]).then_inc(misc_used, 1)

            def out_copy(T):
                act.wait_ge(misc_done, 6 * T + 5)
                if not (isinstance(T, int) and T == 0):
                    act.wait_ge(q_steps, Q_STEPS * (T - 1) + 1)
                nc.scalar.copy(o0[:], psM[:, 0, 0:J]).then_inc(misc_used, 1)

            def ks_copy(T, s):
                act.wait_ge(misc_done, 6 * T + 6)
                act.wait_ge(ks_stored, 16 * T)
                nc.scalar.copy(ks[:], psM[0:BT, 1, 0:J]).then_inc(misc_used, 1)

            def q_cast(T, s, step):
                q, m, r = (qf[:, n, :] for n in range(3))
                if step == 0:
                    act.wait_ge(q_steps, Q_STEPS * T + 1)
                    if not (isinstance(T, int) and T < 2):
                        act.wait_ge(q_stored, 64 * (T - 1))
                    nc.scalar.copy(q_out[:, s, 0, :], q).then_inc(q_casts, 1)
                    nc.scalar.activation(m, q, ACT.Copy, scale=amx[:, bass.ds(T, 1)]).then_inc(q_casts, 1)
                elif step == 1:
                    act.wait_ge(q_steps, Q_STEPS * T + 3)
                    nc.scalar.copy(q_out[:, s, 2, :], m).then_inc(q_casts, 1)
                    nc.scalar.copy(q_out[:, s, 1, :], r).then_inc(q_casts, 1)
                else:
                    act.wait_ge(q_steps, Q_STEPS * T + 5)
                    nc.scalar.copy(q_out[:, s, 3, :], m).then_inc(q_casts, 1)
                    nc.scalar.copy(q_out[:, s, 4, :], r).then_inc(q_casts, 1)

            def z_copy(i, h, n):
                act.wait_ge(z_done, i + 1)
                act.wait_ge(z_stored[h], 16 * FA * n)
                nc.scalar.copy(zS[:, h], psZ[:, 0:2 * G]).then_inc(z_copied, 1)

            def body(t, s, eA, eB, sbk, nx2, nxt):
                T = t + SB_LEAD
                for h in range(2):
                    i = 2 * t + h
                    args = nxt or h == 0
                    e = (2 * s + h + 1) % 4

                    def chunks(*cs):
                        if args:
                            exps(i + 1, e, cs)

                    if eA and h == 1:
                        exp0(t + A_LEAD, s)
                    chunks(0, 1)
                    if h == 0 and nxt:
                        q_cast(t + 1, 1 - s, 1)
                    chunks(2, 3)
                    if sbk and h == 0:
                        chunk_copy(T, 0)
                        chunk_copy(T, 1)
                    if h == 0 and nxt:
                        q_cast(t + 1, 1 - s, 2)
                    chunks(4, 5)
                    if sbk and h == 0:
                        chunk_copy(T, 2)
                        chunk_copy(T, 3)
                    if sbk and h == 1:
                        out_copy(T)
                    chunks(6, 7)
                    if sbk and h == 1:
                        ks_copy(T, s)
                        q_cast(T, s, 0)
                    chunks(8, 9)
                    if not (isinstance(i, int) and i == 0):
                        z_copy(i - 1, h, t if h else t - 1)

            for T in range(A_LEAD):
                exp0(T, T % 2)
                if 1 <= T <= SB_LEAD:
                    for j in range(4):
                        chunk_copy(T - 1, j)
                    out_copy(T - 1)
                    ks_copy(T - 1, T - 1)
                    q_cast(T - 1, T - 1, 0)
                    if T == 1:
                        q_cast(0, 0, 1)
                        q_cast(0, 0, 2)
            exps(0, 0, range(CHUNKS))
            tiles_of(act, body)
            z_copy(2 * TILES - 1, 0, TILES - 1)
            for m in range(B // P * NCH1 // 4):
                act.wait_ge(f_tr, m + 1)
                if m >= 2:
                    act.wait_ge(f_mm, m - 1)
                nc.scalar.copy(y0T[0:CH1, 4 * (m % 2):4 * (m % 2) + 4, :].rearrange("p c n -> p (c n)"),
                               psM[0:CH1, m % 2, :]).then_inc(f_cp, 1)

        @block.gpsimd
        def _(pool):
            def build_a(t, s):
                pool.wait_ge(a_loaded, 32 * (t + 1))
                if not (isinstance(t, int) and t < 2):
                    pool.wait_ge(arg_done, 2 * CHUNKS * (t - 1))
                nc.gpsimd.tensor_tensor(a_diag[:, s],
                                        a_rep[:, s].unsqueeze(2).to_broadcast((P, U * FA, KH, FB)),
                                        dga[:].unsqueeze(1).unsqueeze(3).to_broadcast((P, U * FA, KH, FB)),
                                        ALU.mult).then_inc(a_built, 1)

            def build_v(t, s):
                pool.wait_ge(a_loaded, 32 * (t + 1))
                if not (isinstance(t, int) and t < 2):
                    pool.wait_ge(z_done, 2 * (t - 1))
                xt = xu[:, s].rearrange("p (b h a) -> p h b a", h=2, a=FA)
                vt = v_st[:, s].rearrange("p (b h) a c -> p h b a c", h=2)
                for kh in range(2):
                    for lo, hi, col in ((0, 4, 0), (4, 5, FB)):
                        last = nc.gpsimd.tensor_tensor(vt[:, kh, :, lo:hi, col:col + FB],
                                                       xt[:, kh, :, lo:hi].unsqueeze(3).to_broadcast((P, U // 2, hi - lo, FB)),
                                                       wv_mask[:, kh, lo:hi].unsqueeze(1).to_broadcast((P, U // 2, hi - lo, FB)), ALU.mult)
                last.then_inc(v_built, 1)

            def product0(T, s):
                pool.wait_ge(ew_step, EW_STEPS * T + 3)
                if not (isinstance(T, int) and T < 2):
                    pool.wait_ge(y0_done, T - 1)
                nc.gpsimd.tensor_tensor(arg0[:, s].rearrange("p (f g) -> p f g", f=F), s0[:, s, 0].unsqueeze(2).to_broadcast((P, F, F)),
                                        s0[:, s, 1].unsqueeze(1).to_broadcast((P, F, F)), ALU.mult).then_inc(prod0, 1)

            def weights0(T, s):
                pool.wait_ge(recip0_done, T + 1)
                if not (isinstance(T, int) and T == 0):
                    pool.wait_ge(misc_done, 6 * T - 2)
                nc.gpsimd.tensor_tensor(w0[:].rearrange("p (f g) -> p f g", f=F), s0[:, s, 2].unsqueeze(2).to_broadcast((P, F, F)),
                                        s0[:, s, 5].unsqueeze(1).to_broadcast((P, F, F)), ALU.mult).then_inc(w0_done, 1)

            def apply0(T, s):
                pool.wait_ge(w0_done, T + 1)
                nc.gpsimd.tensor_tensor(w0[:], arg0[:, s], w0[:], ALU.mult).then_inc(y0_done, 1)

            for T in range(A_LEAD):
                product0(T, T % 2)
                if T < EW_LEAD:
                    weights0(T, T % 2)
                    apply0(T, T % 2)
            pool.wait_ge(loaded, 16 * N_CONST)
            nc.gpsimd.memset(v_st[:], 0.0).then_inc(mask_ready, 1)
            for kh in range(2):
                nc.gpsimd.tensor_tensor(wv_mask[:, kh], wvu[:, kh].unsqueeze(2).to_broadcast((P, FA, FB)),
                                        fbm[:].unsqueeze(1).to_broadcast((P, FA, FB)), ALU.mult).then_inc(mask_ready, 1)
            pool.wait_ge(mask_ready, 3)
            build_a(0, 0)
            build_v(0, 0)
            build_a(1, 1)

            def body(t, s, eA, eB, sbk, nx2, nxt):
                if eA:
                    product0(t + A_LEAD, s)
                if eB:
                    weights0(t + EW_LEAD, 1 - s)
                    apply0(t + EW_LEAD, 1 - s)
                if nxt:
                    build_v(t + 1, 1 - s)
                if nx2:
                    build_a(t + 2, s)

            tiles_of(pool, body)

        @block.vector
        def _(dve):
            def w(n, width):
                return w_sb[:, n * F:n * F + width]

            v = nc.vector
            v.memset(minus, -1.0).then_inc(a_split, 1)
            x3 = xr.rearrange("p (t f) -> p t f", f=F)
            a3 = a1.rearrange("p (t f) -> p t f", f=F)

            def prepare(step):
                if step == 0:
                    dve.wait_ge(loaded_x, 16)
                    v.tensor_tensor(a3, x3, w(3, F).unsqueeze(1).to_broadcast((P, TILES, F)), ALU.mult).then_inc(prep, 1)
                    dve.wait_ge(prep, 1)
                    v.tensor_copy(a_hi, a1).then_inc(a_split, 1)
                    v.tensor_reduce(amx[:], a3, AX.X, ALU.max).then_inc(prep, 1)
                elif step == 1:
                    v.tensor_reduce(amn[:], a3, AX.X, ALU.min).then_inc(prep, 1)
                    dve.wait_ge(a_split, 2)
                    dve.wait_ge(prep, 3)
                    v.tensor_tensor(a1, a1, a_hi, ALU.subtract).then_inc(prep, 1)
                elif step == 2:
                    dve.wait_ge(prep, 4)
                    v.tensor_copy(a_md, a1).then_inc(a_split, 1)
                    dve.wait_ge(a_split, 3)
                    v.tensor_tensor(a1, a1, a_md, ALU.subtract).then_inc(prep, 1)
                    dve.wait_ge(prep, 5)
                    v.tensor_copy(a_lo, a1).then_inc(a_split, 1)
                    dve.wait_ge(loaded, 16 * N_CONST)
                    v.tensor_copy(bck[:].rearrange("p u m -> p (u m)"), bck_f).then_inc(bck_ready, 1)

            def ew_products(T, s):
                a0, q0, v0 = (s0[:, s, n] for n in range(3))
                dve.wait_ge(loaded_x0, 16 * (T + 1))
                if not (isinstance(T, int) and T < 2):
                    dve.wait_ge(w0_done, T - 1)
                v.tensor_tensor(a0, xt0[:], w(1, F), ALU.mult).then_inc(ew_step, 1)
                v.tensor_tensor(q0, xt0[:], w(0, F), ALU.mult).then_inc(ew_step, 1)
                v.tensor_tensor(v0, xt0[:], w(2, F), ALU.mult).then_inc(ew_step, 1)
                dve.wait_ge(ew_step, EW_STEPS * T + 3)
                v.tensor_reduce(s0m[:, 0:1], a0, AX.X, ALU.max).then_inc(ew_step, 1)
                v.tensor_reduce(s0m[:, 1:2], a0, AX.X, ALU.min).then_inc(ew_step, 1)

            def ew_max(T, s):
                q0, m0, t0 = s0[:, s, 1], s0[:, s, 3], s0[:, s, 4]
                dve.wait_ge(ew_step, EW_STEPS * T + 5)
                v.tensor_scalar(t0, q0, s0m[:, 0:1], None, ALU.mult).then_inc(ew_step, 1)
                dve.wait_ge(ew_step, EW_STEPS * T + 6)
                v.scalar_tensor_tensor(out=m0, in0=q0, scalar=s0m[:, 1:2], in1=t0, op0=ALU.mult, op1=ALU.max).then_inc(ew_step, 1)

            def ew_shift(T, s):
                dve.wait_ge(ew_step, EW_STEPS * T + 7)
                dve.wait_ge(prod0, T + 1)
                p3 = arg0[:, s].rearrange("p (f g) -> p f g", f=F)
                v.tensor_tensor(p3, p3, s0[:, s, 3].unsqueeze(1).to_broadcast((P, F, F)), ALU.subtract).then_inc(arg0_done, 1)

            def ew_sum(T, s):
                dve.wait_ge(exp0_done, T + 1)
                v.tensor_reduce(s0[:, s, 4], arg0[:, s].rearrange("p (f g) -> p g f", f=F), AX.X, ALU.add).then_inc(sum0_done, 1)
                dve.wait_ge(sum0_done, T + 1)
                v.reciprocal(s0[:, s, 5], s0[:, s, 4]).then_inc(recip0_done, 1)

            def q_stage(T, s, step):
                q, m, r = (qf[:, n, :] for n in range(3))
                at, casts = Q_STEPS * T, Q_CASTS * T
                if step == 0:
                    dve.wait_ge(misc_used, 6 * T + 5)
                    if not (isinstance(T, int) and T == 0):
                        dve.wait_ge(q_casts, casts)
                    v.tensor_tensor(q, o0[:], w(4, G), ALU.mult).then_inc(q_steps, 1)
                elif step == 1:
                    dve.wait_ge(q_casts, casts + 2)
                    v.scalar_tensor_tensor(out=m, in0=q, scalar=amn[:, bass.ds(T, 1)], in1=m, op0=ALU.mult, op1=ALU.max).then_inc(q_steps, 1)
                    v.tensor_tensor(r, q, q_out[:, s, 0, :], ALU.subtract).then_inc(q_steps, 1)
                else:
                    dve.wait_ge(q_casts, casts + 4)
                    v.tensor_tensor(m, m, q_out[:, s, 2, :], ALU.subtract).then_inc(q_steps, 1)
                    v.tensor_tensor(r, r, q_out[:, s, 1, :], ALU.subtract).then_inc(q_steps, 1)

            def recip(i):
                dve.wait_ge(sum_done, i + 1)
                v.reciprocal(rS[:], psS[:, 0:G]).then_inc(recip_done, 1)

            def halve(i):
                dve.wait_ge(recip_done, i + 1)
                v.tensor_copy(r_hi[:], rS[:]).then_inc(hi_done, 1)
                dve.wait_ge(hi_done, i + 1)
                dve.wait_ge(spread_done, 2 * i)
                v.scalar_tensor_tensor(out=r_halves[:], in0=r_hi[:].bitcast(f32), scalar=lo_rows[:], in1=rS[:],
                                       op0=ALU.mult, op1=ALU.add).then_inc(halves_done, 1)

            def normalise(i, p, e):
                dve.wait_ge(spread_done, 2 * i + p + 1)
                x = E[:, e, :, p * 2 * G:(p + 1) * 2 * G]
                v.tensor_tensor(x, x, psB[:, 0:2 * G].unsqueeze(1).to_broadcast((P, FA, 2 * G)), ALU.mult).then_inc(norm_done, 1)

            def body(t, s, eA, eB, sbk, nx2, nxt):
                A, X, Q = t + A_LEAD, t + EW_LEAD, t + SB_LEAD
                i = 2 * t
                prev = not (isinstance(t, int) and t == 0)
                if eA:
                    ew_max(A, s)
                if nxt:
                    q_stage(t + 1, 1 - s, 1)
                if prev:
                    normalise(i - 1, 0, 2 * (1 - s) + 1)
                if nxt:
                    q_stage(t + 1, 1 - s, 2)
                if eB:
                    ew_sum(X, 1 - s)
                if prev:
                    normalise(i - 1, 1, 2 * (1 - s) + 1)
                recip(i)
                halve(i)
                if eA:
                    ew_shift(A, s)
                normalise(i, 0, 2 * s)
                if eA and not (isinstance(A, int) and A + 1 >= TILES):
                    ew_products(A + 1, 1 - s)
                normalise(i, 1, 2 * s)
                recip(i + 1)
                if sbk:
                    q_stage(Q, s, 0)
                halve(i + 1)

            for T in range(A_LEAD):
                if T == 0:
                    dve.wait_ge(loaded_w, 16)
                ew_products(T, T % 2)
                ew_max(T, T % 2)
                if T == 0:
                    prepare(0)
                ew_shift(T, T % 2)
                if T == 0:
                    prepare(1)
                if T < EW_LEAD:
                    ew_sum(T, T % 2)
                if T == 0:
                    prepare(2)
                if 1 <= T <= SB_LEAD:
                    q_stage(T - 1, T - 1, 0)
                    if T == 1:
                        q_stage(0, 0, 1)
                        q_stage(0, 0, 2)
            ew_products(A_LEAD, A_LEAD % 2)
            tiles_of(dve, body)
            for p in range(2):
                normalise(2 * TILES - 1, p, (2 * TILES - 1) % 4)
            for n in range(B // P):
                dve.wait_ge(f_mm, (n + 1) * NCH1 // 4)
                v.tensor_copy(w0[:, n * J:(n + 1) * J], psZ[:, 0:J]).then_inc(f_out, 1)


def kernel(r_inputs, L0_rec_wq0, L0_rec_wk0, L0_rec_wv0, L0_rec_cw0, L0_rec_wq1, L0_rec_wk1, L0_rec_wv1, L0_rec_cw1):
    import numpy as np
    import ml_dtypes
    import concourse.bacc as bacc
    from concourse.bass_utils import run_bass_kernel_spmd

    x = np.asarray(r_inputs)
    c = np.ascontiguousarray
    rows = x.transpose(0, 2, 1).reshape(TILES, P, F)
    x_rows = c(rows.transpose(1, 0, 2).reshape(P, TILES * F))
    x_units = c(x.reshape(TILES, BT, FA, FB, 2, KH).transpose(5, 3, 0, 1, 4, 2).reshape(P, TILES * U * FA))
    w_rows = np.zeros((P, 4 * F + G), np.float32)
    for n, wt in enumerate((L0_rec_wq0, L0_rec_wk0, L0_rec_wv0, L0_rec_wk1, L0_rec_wq1)):
        wt = np.asarray(wt)[0].T
        w_rows[:, n * F:n * F + wt.shape[1]] = np.tile(wt, (BT, 1))
    wv_units = c(np.asarray(L0_rec_wv1)[0].reshape(FA, FB, 2, KH).transpose(3, 1, 2, 0).reshape(P, 2, FA))
    p = np.arange(P)
    ident = np.eye(P, dtype=np.float32)
    diag_a = (p[:, None] // TERMS == np.arange(KH)).astype(np.float32)
    sum_f = (p[:, None] // FB == np.arange(32) % KH).astype(np.float32)
    bcast_k = np.zeros((P, GU, P), np.float32)
    for u in range(GU):
        bcast_k[32 * u + p // FB, u, p] = 1
        bcast_k[32 * u + KH + p // FB, u, p] = 1
    lo_rows = -(p[:, None] % 32 >= KH).astype(np.float32)
    sum_k = (p[:, None] // K == np.arange(32)).astype(np.float32)
    fb_mask = (p[:, None] % FB == np.arange(FB)).astype(np.float32)
    arrays = {
        "x_rows": x_rows, "x_units": x_units, "w_rows": w_rows, "wv_units": wv_units,
        "cw0": c(np.asarray(L0_rec_cw0)[0]), "cw1": c(np.asarray(L0_rec_cw1)[0]),
        "ident_d": ident, "diag_a": diag_a.astype(ml_dtypes.bfloat16), "sum_f": sum_f, "bcast_k": bcast_k,
        "sum_k": sum_k, "lo_rows_d": lo_rows, "fb_mask": fb_mask,
    }
    nc = bacc.Bacc("TRN2", target_bir_lowering=False, num_devices=1)
    args = {n: nc.dram_tensor(n, a.shape, mybir.dt.from_np(a.dtype), kind="ExternalInput").ap() for n, a in arrays.items()}
    out = nc.dram_tensor("out", (B, 2 * J), mybir.dt.float32, kind="ExternalOutput").ap()
    cin_kernel(nc, *args_in_order(args), out)
    r = run_bass_kernel_spmd(nc, [arrays], core_ids=[0])
    return r.results[0]["out"]


def args_in_order(args):
    return [args[n] for n in ("x_rows", "x_units", "w_rows", "wv_units", "cw0", "cw1", "ident_d", "diag_a", "sum_f",
                              "bcast_k", "sum_k", "lo_rows_d", "fb_mask")]
```
